# Optimizing a Trainium2 kernel written in Bass

```python
import numpy as np
import jax
import jax.numpy as jnp

def _softmax(x, axis=-1):
    return jax.nn.softmax(x, axis=axis)

def _gelu(x):
    return jax.nn.gelu(x, approximate=True)

def _silu(x):
    return jax.nn.silu(x)

def _sigmoid(x):
    return jax.nn.sigmoid(x)

def _layernorm(x, axis=-1, eps=1e-05):
    m = jnp.mean(x, axis=axis, keepdims=True)
    v = jnp.var(x, axis=axis, keepdims=True)
    return (x - m) / jnp.sqrt(v + eps)

def _scatter_add(tgt, idx, src, axis=0):
    return tgt.at[idx].add(src)

def _segment_sum(src, seg, n):
    return jax.ops.segment_sum(src, seg, n)
kernel_name = 'mk_adj_resnorm_d4_adj_r2_fe28ea'

def setup_inputs(seed: int=0):
    np.random.seed(seed)
    _w = jnp.asarray

    def _rec_inputs():
        import jax
        import jax.numpy as jnp
        _gk = jax.random.key(seed)
        x = -0.0005207 + 1.001 * jax.random.normal(jax.random.fold_in(_gk, 1), (16, 512, 64), jnp.float32)
        _w = (1.0 + jnp.arange(512, dtype=jnp.float32)) ** (-0.5)
        _w = _w / _w.mean()
        _pij = jnp.clip(0.03125 * _w[:, None] * _w[None, :], 0.0, 1.0)
        _a = jax.random.uniform(jax.random.fold_in(_gk, 2), (16, 512, 512)) < _pij
        _a = jnp.logical_or(_a, jnp.eye(512, dtype=bool))
        _af = _a.astype(jnp.float32)
        _af = _af * jax.random.uniform(jax.random.fold_in(_gk, 3), (16, 512, 512), jnp.float32, 0.05, 1)
        adj = _af
        return (x, adj)
    x, adj = _rec_inputs()

    def _L0_gnn_setup():
        import jax, jax.numpy as jnp
        import numpy as np
        key = jax.random.key(seed)
        k1, k2 = jax.random.split(key)
        B, N, D = (8, 2048, 64)
        x = jax.random.normal(k1, (B, N, D), dtype=jnp.float32)
        A = jax.random.uniform(k2, (B, N, N), dtype=jnp.float32)
        return {'x': x, 'A': A}
    _L0_gnn_all = _L0_gnn_setup()
    _L0_gnn_in = {k: v for k, v in _L0_gnn_all.items() if k in ()}
    del _L0_gnn_all

    def _L1_gnn_setup():
        import jax, jax.numpy as jnp
        import numpy as np
        B, N, F_IN, F_OUT = (32, 1024, 64, 64)
        key = jax.random.key(seed)
        k1, k2, k3 = jax.random.split(key, 3)
        vertices = jax.random.normal(k1, (B, N, F_IN), dtype=jnp.float32)
        g_mat = jax.random.uniform(k2, (B, N, N), dtype=jnp.float32)
        W = jax.random.normal(k3, (F_OUT, F_IN), dtype=jnp.float32) * (1.0 / np.sqrt(F_IN))
        return {'vertices': vertices, 'g_mat': g_mat, 'W': W}
    _L1_gnn_all = _L1_gnn_setup()
    _L1_gnn_in = {k: v for k, v in _L1_gnn_all.items() if k in ('W',)}
    del _L1_gnn_all

    def _L2_gnn_setup():
        import jax, jax.numpy as jnp
        import numpy as np
        K_ORDERS = 4

        def _cheb_forward(inputs, graph, weight, bias):
            B, N, C = inputs.shape
            eye = jnp.eye(N, dtype=graph.dtype)
            d = jnp.sum(graph, axis=-1) ** (-0.5)
            L = eye[None] - d[:, :, None] * graph * d[:, None, :]
            polys = [jnp.broadcast_to(eye, (B, N, N)), L]
            for _ in range(2, K_ORDERS):
                polys.append(2.0 * jnp.matmul(L, polys[-1]) - polys[-2])
            mul_L = jnp.stack(polys[:K_ORDERS], axis=0)
            prop = jnp.einsum('kbnm,bmc->kbnc', mul_L, inputs)
            out = jnp.einsum('kbnc,kcd->bnd', prop, weight[:, 0])
            return out + bias
        key = jax.random.key(seed)
        k1, k2, k3 = jax.random.split(key, 3)
        B, N, C, D = (8, 512, 64, 64)
        inputs = jax.random.normal(k1, (B, N, C), dtype=jnp.float32)
        graph = jax.random.uniform(k2, (B, N, N), dtype=jnp.float32)
        weight = jax.random.normal(k3, (K_ORDERS, 1, C, D), dtype=jnp.float32) * (2.0 / (C + D)) ** 0.5
        bias = jnp.zeros((1, 1, D), dtype=jnp.float32)
        return {'inputs': inputs, 'graph': graph, 'weight': weight, 'bias': bias}
    _L2_gnn_all = _L2_gnn_setup()
    _L2_gnn_in = {k: v for k, v in _L2_gnn_all.items() if k in ('weight', 'bias')}
    del _L2_gnn_all

    def _L3_gnn_setup():
        import jax, jax.numpy as jnp
        import numpy as np
        B, L, F = (8, 2048, 64)
        key = jax.random.key(seed)
        k1, k2, k3, k4 = jax.random.split(key, 4)
        text = jax.random.normal(k1, (B, L, F), dtype=jnp.float32)
        adj = jax.random.uniform(k2, (B, L, L), dtype=jnp.float32)
        weight = jax.random.normal(k3, (F, F), dtype=jnp.float32) * (1.0 / np.sqrt(F))
        bias = jax.random.normal(k4, (F,), dtype=jnp.float32) * 0.01
        return {'text': text, 'adj': adj, 'weight': weight, 'bias': bias}
    _L3_gnn_all = _L3_gnn_setup()
    _L3_gnn_in = {k: v for k, v in _L3_gnn_all.items() if k in ('weight', 'bias')}
    del _L3_gnn_all
    return {'x': x, 'adj': adj, 'L1_gnn_W': _L1_gnn_in['W'], 'L2_gnn_weight': _L2_gnn_in['weight'], 'L2_gnn_bias': _L2_gnn_in['bias'], 'L3_gnn_weight': _L3_gnn_in['weight'], 'L3_gnn_bias': _L3_gnn_in['bias']}

def reference(x, adj, L1_gnn_W, L2_gnn_weight, L2_gnn_bias, L3_gnn_weight, L3_gnn_bias):
    import jax
    import jax.numpy as jnp

    def _L0_gnn_ref(x, A):
        import jax, jax.numpy as jnp
        import numpy as np
        deg = jnp.clip(jnp.sum(A, axis=2, keepdims=True), 1.0, None)
        A_norm = A / deg
        messages = jnp.matmul(A_norm, x)
        return messages

    def _L1_gnn_ref(vertices, g_mat, W):
        import jax, jax.numpy as jnp
        import numpy as np
        B, N, F_IN, F_OUT = (32, 1024, 64, 64)
        agg = jnp.einsum('bnm,bmf->bnf', g_mat, vertices)
        out = jnp.einsum('bnf,of->bno', agg, W)
        return out

    def _L2_gnn_ref(inputs, graph, weight, bias):
        import jax, jax.numpy as jnp
        import numpy as np
        K_ORDERS = 4

        def _cheb_forward(inputs, graph, weight, bias):
            B, N, C = inputs.shape
            eye = jnp.eye(N, dtype=graph.dtype)
            d = jnp.sum(graph, axis=-1) ** (-0.5)
            L = eye[None] - d[:, :, None] * graph * d[:, None, :]
            polys = [jnp.broadcast_to(eye, (B, N, N)), L]
            for _ in range(2, K_ORDERS):
                polys.append(2.0 * jnp.matmul(L, polys[-1]) - polys[-2])
            mul_L = jnp.stack(polys[:K_ORDERS], axis=0)
            prop = jnp.einsum('kbnm,bmc->kbnc', mul_L, inputs)
            out = jnp.einsum('kbnc,kcd->bnd', prop, weight[:, 0])
            return out + bias
        return _cheb_forward(inputs, graph, weight, bias)

    def _L3_gnn_ref(text, adj, weight, bias):
        import jax, jax.numpy as jnp
        import numpy as np
        B, L, F = (8, 2048, 64)
        hidden = jnp.einsum('blf,fo->blo', text, weight)
        out = jnp.einsum('bij,bjo->bio', adj, hidden)
        return out + bias
    x = _layernorm(x + _L0_gnn_ref(x, adj), axis=-1)
    x = _layernorm(x + _L1_gnn_ref(x, adj, L1_gnn_W), axis=-1)
    x = _layernorm(x + _L2_gnn_ref(x, adj, L2_gnn_weight, L2_gnn_bias), axis=-1)
    x = _layernorm(x + _L3_gnn_ref(x, adj, L3_gnn_weight, L3_gnn_bias), axis=-1)
    return x

_drawn_inputs = setup_inputs


def setup_inputs(seed=0):
    import zlib

    import numpy as np

    out = dict(_drawn_inputs(seed))
    spreads = {'L2_gnn_bias': (0.0, 0.1)}
    factors = {'L3_gnn_bias': 8.0}
    for name, (base, spread) in spreads.items():
        noise = np.random.default_rng([zlib.crc32(name.encode()), seed]).standard_normal(out[name].shape)
        drawn = base * np.exp(spread * noise) if base else spread * noise
        out[name] = jnp.asarray(drawn.astype(out[name].dtype))
    for name, factor in factors.items():
        out[name] = (out[name] * factor).astype(out[name].dtype)
    return out
```

```python
import concourse.bass as bass
from concourse import mybir
from contextlib import ExitStack

F32 = mybir.dt.float32
F32R = mybir.dt.float32r
BF16 = mybir.dt.bfloat16
ALU = mybir.AluOpType
ACT = mybir.ActivationFunctionType
AX = mybir.AxisListType

SLOTS = 4
EPS = 1e-5
MEAN, LINEAR, CHEB0, XT, CHEB1, CHEB2, CONV = range(7)
STAGES = 7
NORMS = {MEAN: 0, LINEAR: 1, CHEB2: 2, CONV: 3}
OPERANDS = {MEAN: 0, LINEAR: 1, CHEB0: 2, CHEB1: 3, CHEB2: 4, CONV: 5}
FEEDS = {MEAN: LINEAR, LINEAR: CHEB0, CHEB0: CHEB1, CHEB1: CHEB2, CHEB2: CONV}
PARTS = {MEAN: 0, CHEB0: 1, CHEB1: 2, CHEB2: 3}
JOB_STAGES = (MEAN, LINEAR, CHEB0, CHEB1)


def resnorm_kernel(nc, x, adj, w1, w2, b2, w3, b3, out):
    graphs, nodes, feat = x.shape
    P = 128
    tiles = nodes // P
    jobs = SLOTS * tiles
    groups = graphs // SLOTS
    steps = STAGES * SLOTS
    wide = 2 * feat
    assert wide == P and graphs % SLOTS == 0

    a_view = adj.rearrange("b (t p) m -> b p t m", p=P)
    x_view = x.rearrange("b (t p) f -> b p t f", p=P)
    out_view = out.rearrange("b (t p) f -> b p t f", p=P)

    ctx = ExitStack()
    with ctx:
        def sb(name, shape, dt=F32):
            return ctx.enter_context(nc.sbuf_tensor(name, shape, dt))

        def sem(name):
            return ctx.enter_context(nc.semaphore(name))

        a_rows = [sb(f"a_rows{g}", [P, tiles, nodes]) for g in range(SLOTS)]
        at_hi = sb("at_hi", [P, 2, SLOTS, tiles, nodes], F32R)
        at_lo = sb("at_lo", [P, 2, SLOTS, tiles, nodes], F32R)
        centred = [sb(f"centred{g}", [P, tiles, feat]) for g in range(SLOTS)]
        xf = [sb(f"xf{g}", [P, tiles, feat]) for g in range(SLOTS)]
        xb = [sb(f"xb{g}", [P, tiles, feat]) for g in range(SLOTS)]
        x_over_d = [sb(f"x_over_d{g}", [P, tiles, feat]) for g in range(SLOTS)]
        dx = [sb(f"dx{g}", [P, tiles, feat]) for g in range(SLOTS)]
        operand = [sb(f"operand{g}", [P, tiles, wide], F32R) for g in range(SLOTS)]
        y = [sb(f"y{r}", [P, tiles, feat]) for r in range(2)]
        part = sb("part", [P, tiles, feat])
        square = sb("square", [P, tiles, feat])
        pt_sb = [sb(f"pt_sb{r}", [P, nodes]) for r in range(2)]
        summed = sb("summed", [P, nodes], BF16)
        cols = SLOTS * tiles
        rowsum = sb("rowsum", [P, cols])
        clipped = sb("clipped", [P, cols])
        inv_deg = sb("inv_deg", [P, cols])
        inv_sum = sb("inv_sum", [P, cols])
        d = sb("d", [P, cols])
        inv_d = sb("inv_d", [P, cols])
        feat_sum = sb("feat_sum", [P, cols])
        variance = sb("variance", [P, cols])
        var_eps = sb("var_eps", [P, cols])
        rstd = sb("rstd", [P, cols])
        minus_half = sb("minus_half", [P, cols])
        eps = sb("eps", [P, cols])
        ident = sb("ident", [P, P])
        fold_m = {s: sb(f"fold_m{s}", [P, wide]) for s in OPERANDS}
        fold_v0 = sb("fold_v0", [P, wide])
        w1_rows = sb("w1_rows", [feat, wide])
        w2_sb = sb("w2_sb", [P, 4, feat])
        b2_sb = sb("b2_sb", [P, 1, feat])
        b3_sb = sb("b3_sb", [P, 1, feat])
        w_sum = sb("w_sum", [P, 8])
        w_tmp = sb("w_tmp", [P, 2, feat])

        pt = [ctx.enter_context(nc.psum_tensor(f"pt{r}", [P, nodes], F32)) for r in range(2)]
        turned = [ctx.enter_context(nc.psum_tensor(f"turned{r}", [P, nodes], F32)) for r in range(2)]
        folded = [ctx.enter_context(nc.psum_tensor(f"folded{g}", [P, tiles, wide], F32))
                  for g in range(SLOTS)]

        a_loaded = [sem(f"a_loaded{g}") for g in range(SLOTS)]
        x_loaded = [sem(f"x_loaded{g}") for g in range(SLOTS)]
        xf_free = [sem(f"xf_free{g}") for g in range(SLOTS)]
        weights_loaded = sem("weights_loaded")
        turned_done = sem("turned_done")
        product_done = sem("product_done")
        fold_done = sem("fold_done")
        w1_turned = sem("w1_turned")
        at_hi_done = sem("at_hi_done")
        rows_summed = sem("rows_summed")
        pt_copied = sem("pt_copied")
        squared = sem("squared")
        hi_done = sem("hi_done")
        at_lo_done = sem("at_lo_done")
        feat_summed = sem("feat_summed")
        centred_done = sem("centred_done")
        part_done = sem("part_done")
        y_done = sem("y_done")
        cheb_done = sem("cheb_done")
        variance_done = sem("variance_done")
        norm_done = sem("norm_done")
        dx_done = sem("dx_done")
        lo_done = sem("lo_done")
        clip_done = sem("clip_done")
        stats_done = sem("stats_done")
        setup_done = sem("setup_done")
        ident_started = sem("ident_started")
        ident_done = sem("ident_done")
        var_done = sem("var_done")
        rstd_done = sem("rstd_done")
        biased_done = sem("biased_done")
        over_d_done = sem("over_d_done")
        d_done = sem("d_done")
        inv_d_done = sem("inv_d_done")

        def step_count(i, s, g):
            return i * steps + s * SLOTS + g + 1

        def norm_count(i, s, g):
            return i * (len(NORMS) * SLOTS) + NORMS[s] * SLOTS + g + 1

        def operand_count(i, s, g):
            return i * (len(OPERANDS) * SLOTS) + OPERANDS[s] * SLOTS + g + 1

        def part_count(i, s, g):
            return i * (len(PARTS) * SLOTS) + PARTS[s] * SLOTS + g + 1

        def cheb_count(i, s, g):
            return i * (2 * SLOTS) + (s == CHEB1) * SLOTS + g + 1

        def biased_count(i, s, g):
            return i * (2 * SLOTS) + (s == CHEB2) * SLOTS + g + 1

        def slot_count(i, g):
            return i * SLOTS + g + 1

        def job_count(i, job):
            return i * jobs + job + 1

        def cols_of(t, g):
            return t[:, g * tiles:(g + 1) * tiles]

        def by_row(t, g):
            return cols_of(t, g).unsqueeze(2).broadcast_to([P, tiles, feat])

        def stage_slot(n):
            return n // SLOTS, n % SLOTS

        def job_at(n):
            s, g = stage_slot(n)
            if s not in JOB_STAGES:
                return None
            return JOB_STAGES.index(s) * SLOTS + g

        EYE_V = {CHEB0: 0, CHEB1: 1, CHEB2: 2}
        SETUP_STEPS = 25

        block = ctx.enter_context(nc.Block())

        @block.sync
        def _(sp):
            def load_a(p, g):
                sp.dma_start(a_rows[g][:, :, :], a_view[p * SLOTS + g]).then_inc(a_loaded[g], 16)

            def load_x(p, g):
                sp.dma_start(centred[g][:, :, :], x_view[p * SLOTS + g]).then_inc(x_loaded[g], 16)

            def reload_a(p):
                for g in range(SLOTS):
                    sp.wait_ge(turned_done, job_count(p - 1, g * tiles + tiles - 1))
                    sp.wait_ge(rows_summed, job_count(p - 1, g * tiles + tiles - 1))
                    load_a(p, g)

            def reload_x(p):
                for g in range(SLOTS):
                    sp.wait_ge(y_done, norm_count(p - 1, MEAN, g))
                    load_x(p, g)

            def store(i):
                for g in range(SLOTS):
                    sp.wait_ge(norm_done, norm_count(i, CONV, g))
                    sp.dma_start(out_view[i * SLOTS + g], xf[g][:, :, :]).then_inc(xf_free[g], 16)

            for g in range(SLOTS):
                load_a(0, g)
                load_x(0, g)
            reload_a(1)
            with sp.Fori(0, groups - 2) as i:
                reload_x(i + 1)
                reload_a(i + 2)
                store(i)
            reload_x(groups - 1)
            store(groups - 2)
            store(groups - 1)
            for g in range(SLOTS):
                sp.wait_ge(xf_free[g], 16 * groups + 16)

        @block.tensor
        def _(pe):
            def turn(p, job):
                g, c = job // tiles, job % tiles
                if c == 0:
                    pe.wait_ge(a_loaded[g], 16 * p + 16)
                if not (isinstance(p, int) and p == 0 and job < 2):
                    pe.wait_ge(at_lo_done, job_count(p, job) - 2)
                for t in range(tiles):
                    last = nc.tensor.transpose(turned[job % 2][:, t * P:(t + 1) * P],
                                               a_rows[g][:, t, c * P:(c + 1) * P], ident[:, :])
                last.then_inc(turned_done, 1)

            def product(i, s, g):
                r = g % 2
                if s != MEAN or g >= 2:
                    pe.wait_ge(pt_copied, step_count(i, s, g) - 2)
                if s == XT:
                    pe.wait_ge(over_d_done, slot_count(i, g))
                    for u in range(tiles // 2):
                        last = nc.tensor.transpose(pt[r][:, u * P:(u + 1) * P],
                                                   x_over_d[g][:, 2 * u:2 * u + 2, :], ident[:, :])
                    last.then_inc(product_done, 1)
                    return
                if s == MEAN:
                    pe.wait_ge(at_lo_done, job_count(i, g * tiles + tiles - 1))
                pe.wait_ge(lo_done, operand_count(i, s, g))
                for c in range(tiles):
                    for a in (at_hi, at_lo):
                        last = nc.tensor.matmul(pt[r][:, :], operand[g][:, c, :], a[:, i % 2, g, c, :],
                                                start=(c == 0 and a is at_hi),
                                                stop=(c == tiles - 1 and a is at_lo))
                last.then_inc(product_done, 1)

            def fold(i, s, g):
                r = g % 2
                pe.wait_ge(pt_copied, step_count(i, s, g))
                if s == XT:
                    pe.wait_ge(part_done, part_count(i, CHEB0, g))
                    for u in range(tiles // 2):
                        last = nc.tensor.matmul(folded[g][:, 2 * u:2 * u + 2, feat:wide],
                                                pt_sb[r][:, u * P:(u + 1) * P], fold_v0[:, :],
                                                start=False, stop=False, skip_group_check=True)
                    last.then_inc(fold_done, 1)
                    return
                for t in range(tiles):
                    last = nc.tensor.matmul(folded[g][:, t, :], pt_sb[r][:, t * P:(t + 1) * P],
                                            fold_m[s][:, :],
                                            start=(t == 0 and s not in (CHEB1, CHEB2)),
                                            stop=(t == tiles - 1), skip_group_check=True)
                last.then_inc(fold_done, 1)

            pe.wait_ge(ident_done, 1)
            pe.wait_ge(weights_loaded, 16 * 8)
            nc.tensor.transpose(pt[0][:, 0:feat], w1_rows[:, :], ident[0:feat, 0:feat]).then_inc(w1_turned, 1)
            for job in range(jobs):
                turn(0, job)
            pe.wait_ge(setup_done, SETUP_STEPS)

            def group(i, last_group):
                for n in range(steps):
                    s, g = stage_slot(n)
                    product(i, s, g)
                    if job_at(n) is not None and not last_group:
                        turn(i + 1, job_at(n))
                    if n > 0:
                        fold(i, *stage_slot(n - 1))
                fold(i, *stage_slot(steps - 1))

            with pe.Fori(0, groups - 1) as i:
                group(i, False)
            group(groups - 1, True)

        @block.scalar
        def _(act):
            act.dma_start(w1_rows[:, 0:feat], w1).then_inc(weights_loaded, 16)
            act.dma_start(w1_rows[:, feat:wide], w1).then_inc(weights_loaded, 16)
            for half in (0, feat):
                act.dma_start(w2_sb[half:half + feat, :, :],
                              w2.rearrange("k o c d -> c (k o) d")).then_inc(weights_loaded, 16)
                act.dma_start(fold_m[CONV][half:half + feat, 0:feat], w3).then_inc(weights_loaded, 16)
            act.dma_start(b2_sb[:, 0, :], b2[0, 0, :].partition_broadcast(P)).then_inc(weights_loaded, 16)
            act.dma_start(b3_sb[:, 0, :], b3.partition_broadcast(P)).then_inc(weights_loaded, 16)

            def turned_hi(p, job):
                g, c = job // tiles, job % tiles
                act.wait_ge(turned_done, job_count(p, job))
                nc.scalar.activation(at_hi[:, p % 2, g, c, :], turned[job % 2][:, :],
                                     ACT.Copy).then_inc(at_hi_done, 1)

            def sum_rows(p, job):
                g, t = job // tiles, job % tiles
                if t == 0:
                    act.wait_ge(a_loaded[g], 16 * p + 16)
                if g == 0 and t == 0:
                    act.wait_ge(stats_done, p)
                    act.wait_ge(inv_d_done, p)
                if not (isinstance(p, int) and p == 0 and job == 0):
                    act.wait_ge(rows_summed, job_count(p, job) - 1)
                nc.scalar.activation(summed[:, :], a_rows[g][:, t, :], ACT.Copy,
                                     accum_out=rowsum[:, job:job + 1]).then_inc(rows_summed, 1)

            def copy_pt(i, s, g):
                r = g % 2
                act.wait_ge(product_done, step_count(i, s, g))
                if s != MEAN or g >= 2:
                    act.wait_ge(fold_done, step_count(i, s, g) - 2)
                n = nodes if s != XT else tiles // 2 * P
                nc.scalar.activation(pt_sb[r][:, 0:n], pt[r][:, 0:n], ACT.Copy).then_inc(pt_copied, 1)

            def square_y(i, s, g):
                act.wait_ge(y_done, norm_count(i, s, g))
                nc.scalar.activation(square[:, :, :], y[g % 2][:, :, :], ACT.Square,
                                     scale=feat ** -0.5).then_inc(squared, 1)

            def hi_first(p, g):
                act.wait_ge(centred_done, slot_count(p, g))
                if not isinstance(p, int):
                    act.wait_ge(product_done, step_count(p - 1, CONV, g))
                nc.scalar.activation(operand[g][:, :, 0:feat], centred[g][:, :, :],
                                     ACT.Copy).then_inc(hi_done, 1)

            def hi(i, s, g):
                if s == LINEAR:
                    act.wait_ge(dx_done, slot_count(i, g))
                    src = dx[g]
                elif s in (CHEB0, CHEB1):
                    act.wait_ge(cheb_done, cheb_count(i, s, g))
                    src = xf[g]
                else:
                    act.wait_ge(norm_done, norm_count(i, s, g))
                    src = xf[g]
                act.wait_ge(product_done, step_count(i, s, g))
                nc.scalar.activation(operand[g][:, :, 0:feat], src[:, :, :], ACT.Copy).then_inc(hi_done, 1)

            for g in range(SLOTS):
                hi_first(0, g)
            for job in range(jobs):
                turned_hi(0, job)
                sum_rows(0, job)

            def group(i, last_group):
                def incoming(n):
                    copy_pt(i, *stage_slot(n))
                    if job_at(n) is not None and not last_group:
                        turned_hi(i + 1, job_at(n))

                incoming(0)
                incoming(1)
                for n in range(steps):
                    s, g = stage_slot(n)
                    if n > 0:
                        before = stage_slot(n - 1)
                        if before[0] in FEEDS:
                            hi(i, *before)
                    if s in NORMS:
                        square_y(i, s, g)
                    if s == CONV and not last_group:
                        hi_first(i + 1, g)
                    if job_at(n) is not None and not last_group:
                        sum_rows(i + 1, job_at(n))
                    if n + 2 < steps:
                        incoming(n + 2)

            with act.Fori(0, groups - 1) as i:
                group(i, False)
            group(groups - 1, True)

        @block.vector
        def _(dve):
            count = [0]

            def setup(ins):
                count[0] += 1
                ins.then_inc(setup_done, 1)
                dve.wait_ge(setup_done, count[0])

            def sum_feat(p, g):
                dve.wait_ge(x_loaded[g], 16 * p + 16)
                nc.vector.tensor_reduce(cols_of(feat_sum, g), centred[g][:, :, :], AX.X, ALU.add)\
                    .then_inc(feat_summed, 1)

            def centre(p, g):
                dve.wait_ge(feat_summed, slot_count(p, g))
                nc.vector.scalar_tensor_tensor(centred[g][:, :, :], by_row(feat_sum, g), -1.0 / feat,
                                               centred[g][:, :, :], ALU.mult, ALU.add)\
                    .then_inc(centred_done, 1)

            def lo_first(p, g):
                dve.wait_ge(hi_done, operand_count(p, MEAN, g))
                nc.vector.tensor_tensor(operand[g][:, :, feat:wide], centred[g][:, :, :],
                                        operand[g][:, :, 0:feat].bitcast(F32), ALU.subtract)\
                    .then_inc(lo_done, 1)

            def turned_lo(p, job):
                g, c = job // tiles, job % tiles
                dve.wait_ge(at_hi_done, job_count(p, job))
                nc.vector.tensor_tensor(at_lo[:, p % 2, g, c, :], turned[job % 2][:, :],
                                        at_hi[:, p % 2, g, c, :].bitcast(F32), ALU.subtract)\
                    .then_inc(at_lo_done, 1)

            def clip(p):
                dve.wait_ge(rows_summed, job_count(p, jobs - 1))
                nc.vector.tensor_scalar(clipped[:, :], rowsum[:, :], 1.0, None, ALU.max).then_inc(clip_done, 1)

            def invert(p):
                dve.wait_ge(clip_done, p + 1)
                nc.vector.reciprocal(inv_deg[:, :], clipped[:, :])
                nc.vector.reciprocal(inv_sum[:, :], rowsum[:, :]).then_inc(stats_done, 1)

            def read_fold(i, s, g):
                own = folded[g][:, :, 0:feat]
                if (s, g) == (CHEB2, 0):
                    dve.wait_ge(cheb_done, cheb_count(i, CHEB1, SLOTS - 1))
                elif s == CHEB1 or s == CHEB0 and g > 0:
                    dve.wait_ge(cheb_done, cheb_count(i, s, g) - 1)
                elif s in (MEAN, CHEB2) and g > 0:
                    dve.wait_ge(y_done, norm_count(i, s, g) - 1)
                dve.wait_ge(fold_done, step_count(i, s, g))
                if s == MEAN:
                    dve.wait_ge(stats_done, i + 1)
                    nc.vector.tensor_tensor(part[:, :, :], own, by_row(inv_deg, g), ALU.mult)\
                        .then_inc(part_done, 1)
                    residual = centred[g]
                elif s in (CHEB0, CHEB1):
                    factor = -1.0 if s == CHEB0 else -2.0
                    nc.vector.scalar_tensor_tensor(part[:, :, :], own, factor, by_row(inv_sum, g),
                                                   ALU.mult, ALU.mult).then_inc(part_done, 1)
                    dve.wait_ge(part_done, part_count(i, s, g))
                    if s == CHEB0:
                        dve.wait_ge(biased_done, biased_count(i, LINEAR, g))
                        dve.wait_ge(over_d_done, slot_count(i, g))
                    nc.vector.tensor_tensor(xf[g][:, :, :], part[:, :, :], dx[g][:, :, :], ALU.add)\
                        .then_inc(cheb_done, 1)
                    return
                elif s == CHEB2:
                    nc.vector.scalar_tensor_tensor(part[:, :, :], folded[g][:, :, feat:wide], -1.0,
                                                   by_row(d, g), ALU.mult, ALU.mult).then_inc(part_done, 1)
                    residual = xb[g]
                elif s == LINEAR:
                    residual = xf[g]
                else:
                    dve.wait_ge(biased_done, biased_count(i, CHEB2, g))
                    residual = xb[g]
                if s in (MEAN, CHEB2):
                    dve.wait_ge(part_done, part_count(i, s, g))
                    own = part[:, :, :]
                nc.vector.tensor_tensor(y[g % 2][:, :, :], own, residual[:, :, :], ALU.add)\
                    .then_inc(y_done, 1)

            def sum_squares(i, s, g):
                dve.wait_ge(squared, norm_count(i, s, g))
                nc.vector.tensor_reduce(cols_of(variance, g), square[:, :, :], AX.X, ALU.add)\
                    .then_inc(variance_done, 1)

            def normalise(i, s, g):
                dve.wait_ge(rstd_done, norm_count(i, s, g))
                if s == MEAN:
                    dve.wait_ge(xf_free[g], 16 * i + 16)
                nc.vector.tensor_tensor(xf[g][:, :, :], y[g % 2][:, :, :], by_row(rstd, g), ALU.mult)\
                    .then_inc(norm_done, 1)
                if s == LINEAR:
                    dve.wait_ge(norm_done, norm_count(i, s, g))
                    dve.wait_ge(d_done, i + 1)
                    nc.vector.tensor_tensor(dx[g][:, :, :], xf[g][:, :, :], by_row(d, g), ALU.mult)\
                        .then_inc(dx_done, 1)

            def lo(i, s, g):
                dve.wait_ge(hi_done, operand_count(i, FEEDS[s], g))
                src = dx[g] if s == LINEAR else xf[g]
                nc.vector.tensor_tensor(operand[g][:, :, feat:wide], src[:, :, :],
                                        operand[g][:, :, 0:feat].bitcast(F32), ALU.subtract)\
                    .then_inc(lo_done, 1)

            for g in range(SLOTS):
                nc.vector.memset(xf[g][:, 0, 0:1], 0.0).then_inc(xf_free[g], 16)
            setup(nc.vector.memset(minus_half[:, :], -0.5))
            setup(nc.vector.memset(eps[:, :], EPS))
            for s in (MEAN, LINEAR, CONV):
                setup(nc.vector.memset(fold_m[s][:, feat:wide], 0.0))
            setup(nc.vector.memset(fold_v0[:, :], 0.0))
            for g in range(SLOTS):
                sum_feat(0, g)
                centre(0, g)
            for g in range(SLOTS):
                lo_first(0, g)
            dve.wait_ge(ident_done, 1)
            for s in (MEAN, CHEB0, CHEB1, CHEB2):
                setup(nc.vector.tensor_tensor(fold_m[s][:, 0:feat], ident[:, 0:feat], ident[:, feat:wide],
                                              ALU.add))
            dve.wait_ge(weights_loaded, 16 * 8)
            dve.wait_ge(w1_turned, 1)
            w1_t = fold_m[LINEAR][:, 0:feat]
            w3_c = fold_m[CONV][:, 0:feat]
            setup(nc.vector.tensor_copy(w1_t, pt[0][:, 0:feat]))
            nc.vector.tensor_reduce(w_sum[:, 0:4], w2_sb[:, :, :], AX.X, ALU.add)
            nc.vector.tensor_reduce(w_sum[:, 4:5], w1_t, AX.X, ALU.add)
            nc.vector.tensor_reduce(w_sum[:, 5:6], w3_c, AX.X, ALU.add)
            nc.vector.tensor_reduce(w_sum[:, 6:7], b2_sb[:, 0, :], AX.X, ALU.add)
            setup(nc.vector.tensor_reduce(w_sum[:, 7:8], b3_sb[:, 0, :], AX.X, ALU.add))
            setup(nc.vector.scalar_tensor_tensor(w2_sb[:, :, :], w_sum[:, 0:4].unsqueeze(2).broadcast_to([P, 4, feat]),
                                                 -1.0 / feat, w2_sb[:, :, :], ALU.mult, ALU.add))
            for n, w in enumerate((w1_t, w3_c, b2_sb[:, 0, :], b3_sb[:, 0, :])):
                setup(nc.vector.scalar_tensor_tensor(w, w_sum[:, 4 + n:5 + n].broadcast_to([P, feat]),
                                                     -1.0 / feat, w, ALU.mult, ALU.add))
            w_k = [w2_sb[:, k, :] for k in range(4)]
            v1, v2, v3 = (fold_m[s][:, feat:wide] for s in (CHEB0, CHEB1, CHEB2))
            setup(nc.vector.tensor_scalar(v3, w_k[3], 2.0, None, ALU.mult))
            setup(nc.vector.scalar_tensor_tensor(v2, w_k[3], 2.0, w_k[2], ALU.mult, ALU.add))
            setup(nc.vector.tensor_scalar(v2, v2, 2.0, None, ALU.mult))
            setup(nc.vector.scalar_tensor_tensor(w_tmp[:, 0, :], w_k[3], 3.0, w_k[1], ALU.mult, ALU.add))
            setup(nc.vector.scalar_tensor_tensor(v1, w_k[2], 2.0, w_tmp[:, 0, :], ALU.mult, ALU.add))
            setup(nc.vector.tensor_tensor(w_tmp[:, 0, :], w_k[0], w_k[1], ALU.add))
            setup(nc.vector.tensor_tensor(w_tmp[:, 1, :], w_k[2], w_k[3], ALU.add))
            for h in range(2):
                rows = slice(h * feat, (h + 1) * feat)
                ins = nc.vector.scalar_tensor_tensor(fold_v0[rows, rows], w_tmp[rows, 0, :], -1.0,
                                                     w_tmp[rows, 1, :], ALU.mult, ALU.subtract)
            setup(ins)
            assert count[0] == SETUP_STEPS, count[0]
            for job in range(jobs):
                turned_lo(0, job)
            clip(0)
            invert(0)

            def group(i, last_group):
                def split_job(n):
                    if n < steps and job_at(n) is not None and not last_group:
                        turned_lo(i + 1, job_at(n))

                split_job(0)
                for n in range(steps):
                    s, g = stage_slot(n)
                    before = stage_slot(n - 1) if n > 0 else (None, None)
                    if before[0] in NORMS:
                        normalise(i, *before)
                    if s != XT:
                        read_fold(i, s, g)
                    if before[0] in FEEDS:
                        lo(i, *before)
                    if s == CONV and not last_group and g > 0:
                        lo_first(i + 1, g - 1)
                    split_job(n + 1)
                    if s in NORMS:
                        sum_squares(i, s, g)
                    if s == CHEB2 and not last_group:
                        sum_feat(i + 1, g)
                        centre(i + 1, g)
                    if (s, g) == (CONV, 0) and not last_group:
                        clip(i + 1)
                        invert(i + 1)
                normalise(i, CONV, SLOTS - 1)
                if not last_group:
                    lo_first(i + 1, SLOTS - 1)

            with dve.Fori(0, groups - 1) as i:
                group(i, False)
            group(groups - 1, True)

        @block.gpsimd
        def _(pool):
            nc.gpsimd.memset(ident[:, :], 0.0).then_inc(ident_started, 1)
            pool.wait_ge(ident_started, 1)
            nc.gpsimd.affine_select(out=ident[:, :], in_=ident[:, :], compare_op=ALU.not_equal, fill=1.0,
                                    base=0, pattern=[[-1, P]], channel_multiplier=1).then_inc(ident_done, 1)

            def root(p):
                pool.wait_ge(rows_summed, job_count(p, jobs - 1))
                if not isinstance(p, int) or p:
                    pool.wait_ge(part_done, p * (len(PARTS) * SLOTS))
                nc.gpsimd.tensor_tensor(d[:, :], rowsum[:, :], minus_half[:, :], ALU.pow).then_inc(d_done, 1)
                pool.wait_ge(d_done, p + 1)
                nc.gpsimd.tensor_tensor(inv_d[:, :], rowsum[:, :], d[:, :], ALU.mult).then_inc(inv_d_done, 1)

            def root_var(i, s, g):
                pool.wait_ge(variance_done, norm_count(i, s, g))
                nc.gpsimd.tensor_tensor(cols_of(var_eps, g), cols_of(variance, g), cols_of(eps, g),
                                        ALU.add).then_inc(var_done, 1)
                pool.wait_ge(var_done, norm_count(i, s, g))
                nc.gpsimd.tensor_tensor(cols_of(rstd, g), cols_of(var_eps, g), cols_of(minus_half, g),
                                        ALU.pow).then_inc(rstd_done, 1)

            def add_bias(i, s, g):
                bias = b2_sb if s == LINEAR else b3_sb
                pool.wait_ge(norm_done, norm_count(i, s, g))
                nc.gpsimd.tensor_tensor(xb[g][:, :, :], xf[g][:, :, :], bias[:, :, :].broadcast_to([P, tiles, feat]),
                                        ALU.add).then_inc(biased_done, 1)

            def over_d(i, g):
                pool.wait_ge(norm_done, norm_count(i, LINEAR, g))
                pool.wait_ge(inv_d_done, i + 1)
                nc.gpsimd.tensor_tensor(x_over_d[g][:, :, :], xf[g][:, :, :], by_row(inv_d, g), ALU.mult)\
                    .then_inc(over_d_done, 1)

            pool.wait_ge(setup_done, SETUP_STEPS)
            root(0)

            def group(i, last_group):
                for n in range(steps):
                    s, g = stage_slot(n)
                    before = stage_slot(n - 1) if n > 0 else (None, None)
                    if before[0] == LINEAR:
                        over_d(i, before[1])
                        add_bias(i, *before)
                    if before[0] == CHEB2:
                        add_bias(i, *before)
                    if s in NORMS:
                        root_var(i, s, g)
                    if (s, g) == (CONV, 0) and not last_group:
                        root(i + 1)

            with pool.Fori(0, groups - 1) as i:
                group(i, False)
            group(groups - 1, True)


_INS = ['x', 'adj', 'L1_gnn_W', 'L2_gnn_weight', 'L2_gnn_bias', 'L3_gnn_weight', 'L3_gnn_bias']
_OUTS = [((16, 512, 64), 'float32')]


def kernel(**inputs):
    import numpy as _np
    import concourse.bacc as _bacc
    from concourse import mybir as _mybir
    from concourse.bass_utils import run_bass_kernel_spmd as _run

    nc = _bacc.Bacc("TRN2", target_bir_lowering=False, num_devices=1)
    arrays, args = {}, []
    for name in _INS:
        a = _np.ascontiguousarray(inputs[name])
        arrays[f"in_{name}_dram"] = a
        args.append(nc.dram_tensor(f"in_{name}_dram", a.shape, _mybir.dt.from_np(a.dtype), kind="ExternalInput").ap())
    for i, (shape, dtype) in enumerate(_OUTS):
        dt = _mybir.dt.from_np(_np.dtype(dtype))
        args.append(nc.dram_tensor(f"out_{i}_dram", shape, dt, kind="ExternalOutput").ap())
    resnorm_kernel(nc, *args)
    r = _run(nc, [arrays], core_ids=[0])
    got = tuple(r.results[0][f"out_{i}_dram"] for i in range(len(_OUTS)))
    return got[0]
```

```python
import concourse.bass as bass
from concourse import mybir
from contextlib import ExitStack

F32 = mybir.dt.float32
F32R = mybir.dt.float32r
BF16 = mybir.dt.bfloat16
ALU = mybir.AluOpType
ACT = mybir.ActivationFunctionType
AX = mybir.AxisListType

SLOTS = 4
EPS = 1e-5
MEAN, LINEAR, CHEB0, XT, CHEB1, CHEB2, CONV = range(7)
STAGES = 7
NORMS = {MEAN: 0, LINEAR: 1, CHEB2: 2, CONV: 3}
OPERANDS = {MEAN: 0, LINEAR: 1, CHEB0: 2, CHEB1: 3, CHEB2: 4, CONV: 5}
FEEDS = {MEAN: LINEAR, LINEAR: CHEB0, CHEB0: CHEB1, CHEB1: CHEB2, CHEB2: CONV}
PARTS = {MEAN: 0, CHEB0: 1, CHEB1: 2, CHEB2: 3}
SUM_STAGES = (LINEAR, CHEB0, CHEB1, CHEB2)
JOB_STAGES = (LINEAR, CHEB0, XT, CHEB1)


def resnorm_kernel(nc, x, adj, w1, w2, b2, w3, b3, out):
    graphs, nodes, feat = x.shape
    P = 128
    tiles = nodes // P
    jobs = SLOTS * tiles
    groups = graphs // SLOTS
    steps = STAGES * SLOTS
    wide = 2 * feat
    assert wide == P and graphs % SLOTS == 0

    a_view = adj.rearrange("b (t p) m -> b p t m", p=P)
    x_view = x.rearrange("b (t p) f -> b p t f", p=P)
    out_view = out.rearrange("b (t p) f -> b p t f", p=P)

    ctx = ExitStack()
    with ctx:
        def sb(name, shape, dt=F32):
            return ctx.enter_context(nc.sbuf_tensor(name, shape, dt))

        def sem(name):
            return ctx.enter_context(nc.semaphore(name))

        a_rows = [sb(f"a_rows{g}", [P, tiles, nodes]) for g in range(SLOTS)]
        at_hi = sb("at_hi", [P, 2, SLOTS, tiles, nodes], F32R)
        at_lo = sb("at_lo", [P, 2, SLOTS, tiles, nodes], F32R)
        centred = [sb(f"centred{g}", [P, tiles, feat]) for g in range(SLOTS)]
        xf = [sb(f"xf{g}", [P, tiles, feat]) for g in range(SLOTS)]
        xb = [sb(f"xb{g}", [P, tiles, feat]) for g in range(SLOTS)]
        x_over_d = [sb(f"x_over_d{g}", [P, tiles, feat]) for g in range(SLOTS)]
        dx = [sb(f"dx{g}", [P, tiles, feat]) for g in range(SLOTS)]
        operand = [sb(f"operand{g}", [P, tiles, wide], F32R) for g in range(SLOTS)]
        y = [sb(f"y{g}", [P, tiles, feat]) for g in range(SLOTS)]
        part = sb("part", [P, tiles, feat])
        hi_plus_lo = sb("hi_plus_lo", [P, tiles, feat])
        square = sb("square", [P, tiles, feat])
        pt_sb = [sb(f"pt_sb{r}", [P, nodes]) for r in range(2)]
        summed = sb("summed", [P, nodes], BF16)
        cols = SLOTS * tiles
        rowsum = sb("rowsum", [P, cols])
        clipped = sb("clipped", [P, cols])
        inv_deg = sb("inv_deg", [P, cols])
        inv_sum = sb("inv_sum", [P, cols])
        d = sb("d", [P, cols])
        inv_d = sb("inv_d", [P, cols])
        feat_sum = sb("feat_sum", [P, cols])
        variance = sb("variance", [P, cols])
        var_eps = sb("var_eps", [P, cols])
        rstd = sb("rstd", [P, cols])
        minus_half = sb("minus_half", [P, cols])
        eps = sb("eps", [P, cols])
        ident = sb("ident", [P, P])
        fold_m = {s: sb(f"fold_m{s}", [P, wide]) for s in OPERANDS if s != MEAN}
        fold_v0 = sb("fold_v0", [P, wide])
        w1_rows = sb("w1_rows", [feat, wide])
        w2_sb = sb("w2_sb", [P, 4, feat])
        b2_sb = sb("b2_sb", [P, 1, feat])
        b3_sb = sb("b3_sb", [P, 1, feat])
        w_sum = sb("w_sum", [P, 8])
        w_tmp = sb("w_tmp", [P, 2, feat])

        pt = [ctx.enter_context(nc.psum_tensor(f"pt{r}", [P, nodes], F32)) for r in range(2)]
        turned = [ctx.enter_context(nc.psum_tensor(f"turned{r}", [P, nodes], F32)) for r in range(2)]
        folded_banks = [ctx.enter_context(nc.psum_tensor(f"folded{g}", [P, nodes], F32))
                        for g in range(SLOTS)]
        folded = [bank[:, :].rearrange("p (t c) -> p t c", c=wide) for bank in folded_banks]

        first_banks = (turned[0], turned[1], folded_banks[2], folded_banks[3])

        a_loaded = [sem(f"a_loaded{g}") for g in range(SLOTS)]
        x_loaded = [sem(f"x_loaded{g}") for g in range(SLOTS)]
        xf_free = [sem(f"xf_free{g}") for g in range(SLOTS)]
        weights_loaded = sem("weights_loaded")
        turned_done = sem("turned_done")
        product_done = sem("product_done")
        fold_done = sem("fold_done")
        w1_turned = sem("w1_turned")
        at_hi_done = sem("at_hi_done")
        rows_summed = sem("rows_summed")
        pt_copied = sem("pt_copied")
        squared = sem("squared")
        hi_done = sem("hi_done")
        at_lo_done = sem("at_lo_done")
        feat_summed = sem("feat_summed")
        centred_done = sem("centred_done")
        halves_added = sem("halves_added")
        part_done = sem("part_done")
        y_done = sem("y_done")
        cheb_done = sem("cheb_done")
        variance_done = sem("variance_done")
        norm_done = sem("norm_done")
        dx_done = sem("dx_done")
        lo_done = sem("lo_done")
        clip_done = sem("clip_done")
        stats_done = sem("stats_done")
        w1_copied = sem("w1_copied")
        eyes_done = sem("eyes_done")
        setup_done = sem("setup_done")
        ident_started = sem("ident_started")
        ident_done = sem("ident_done")
        var_done = sem("var_done")
        rstd_done = sem("rstd_done")
        biased_done = sem("biased_done")
        over_d_done = sem("over_d_done")
        d_done = sem("d_done")
        inv_d_done = sem("inv_d_done")

        def step_count(i, s, g):
            return i * steps + s * SLOTS + g + 1

        def norm_count(i, s, g):
            return i * (len(NORMS) * SLOTS) + NORMS[s] * SLOTS + g + 1

        def operand_count(i, s, g):
            return i * (len(OPERANDS) * SLOTS) + OPERANDS[s] * SLOTS + g + 1

        def part_count(i, s, g):
            return i * (len(PARTS) * SLOTS) + PARTS[s] * SLOTS + g + 1

        def cheb_count(i, s, g):
            return i * (2 * SLOTS) + (s == CHEB1) * SLOTS + g + 1

        def biased_count(i, s, g):
            return i * (2 * SLOTS) + (s == CHEB2) * SLOTS + g + 1

        def slot_count(i, g):
            return i * SLOTS + g + 1

        def job_count(i, job):
            return i * jobs + job + 1

        def cols_of(t, g):
            return t[:, g * tiles:(g + 1) * tiles]

        def by_row(t, g):
            return cols_of(t, g).unsqueeze(2).broadcast_to([P, tiles, feat])

        def steps_of(i, last_group):
            own = [(i, s, g) for s in range(LINEAR, STAGES) for g in range(SLOTS)]
            return own if last_group else own + [(i + 1, MEAN, g) for g in range(SLOTS)]

        def job_at(s, g, last_group, stages=JOB_STAGES):
            if last_group or s not in stages:
                return None
            return stages.index(s) * SLOTS + g

        EYES = (CHEB0, CHEB1, CHEB2)
        SETUP_STEPS = 19

        block = ctx.enter_context(nc.Block())

        @block.sync
        def _(sp):
            def load_a(p, g):
                sp.dma_start(a_rows[g][:, :, :], a_view[p * SLOTS + g]).then_inc(a_loaded[g], 16)

            def load_x(p, g):
                sp.dma_start(centred[g][:, :, :], x_view[p * SLOTS + g]).then_inc(x_loaded[g], 16)

            def reload_a(p):
                for g in range(SLOTS):
                    sp.wait_ge(turned_done, job_count(p - 1, g * tiles + tiles - 1))
                    sp.wait_ge(rows_summed, job_count(p - 1, g * tiles + tiles - 1))
                    load_a(p, g)

            def reload_x(p):
                for g in range(SLOTS):
                    sp.wait_ge(y_done, norm_count(p - 1, MEAN, g))
                    load_x(p, g)

            def store(i):
                for g in range(SLOTS):
                    sp.wait_ge(norm_done, norm_count(i, CONV, g))
                    sp.dma_start(out_view[i * SLOTS + g], xf[g][:, :, :]).then_inc(xf_free[g], 16)

            sp.dma_start(w1_rows[:, 0:feat], w1).then_inc(weights_loaded, 16)
            sp.dma_start(w1_rows[:, feat:wide], w1).then_inc(weights_loaded, 16)
            for half in (0, feat):
                sp.dma_start(w2_sb[half:half + feat, :, :],
                              w2.rearrange("k o c d -> c (k o) d")).then_inc(weights_loaded, 16)
                sp.dma_start(fold_m[CONV][half:half + feat, 0:feat], w3).then_inc(weights_loaded, 16)
            sp.dma_start(b2_sb[:, 0, :], b2[0, 0, :].partition_broadcast(P)).then_inc(weights_loaded, 16)
            sp.dma_start(b3_sb[:, 0, :], b3.partition_broadcast(P)).then_inc(weights_loaded, 16)
            for g in range(SLOTS):
                load_x(0, g)
                load_a(0, g)
            reload_a(1)
            with sp.Fori(0, groups - 2) as i:
                reload_x(i + 1)
                reload_a(i + 2)
                store(i)
            reload_x(groups - 1)
            store(groups - 2)
            store(groups - 1)
            for g in range(SLOTS):
                sp.wait_ge(xf_free[g], 16 * groups + 16)

        @block.tensor
        def _(pe):
            def turn(p, job, banks=turned):
                g, c = job // tiles, job % tiles
                bank = banks[job % len(banks)]
                if c == 0:
                    pe.wait_ge(a_loaded[g], 16 * p + 16)
                if not isinstance(p, int) or job >= len(banks):
                    pe.wait_ge(at_lo_done, job_count(p, job) - len(banks))
                for t in range(tiles):
                    last = nc.tensor.transpose(bank[:, t * P:(t + 1) * P],
                                               a_rows[g][:, t, c * P:(c + 1) * P], ident[:, :])
                last.then_inc(turned_done, 1)

            def product(i, s, g):
                r = g % 2
                if not isinstance(i, int) or s != MEAN or g >= 2:
                    pe.wait_ge(pt_copied, step_count(i, s, g) - 2)
                if s == XT:
                    pe.wait_ge(over_d_done, slot_count(i, g))
                    for u in range(tiles // 2):
                        last = nc.tensor.transpose(pt[r][:, u * P:(u + 1) * P],
                                                   x_over_d[g][:, 2 * u:2 * u + 2, :], ident[:, :])
                    last.then_inc(product_done, 1)
                    return
                if s == MEAN:
                    pe.wait_ge(at_lo_done, job_count(i, g * tiles + tiles - 1))
                pe.wait_ge(lo_done, operand_count(i, s, g))
                for c in range(tiles):
                    for a in (at_hi, at_lo):
                        last = nc.tensor.matmul(pt[r][:, :], operand[g][:, c, :], a[:, i % 2, g, c, :],
                                                start=(c == 0 and a is at_hi),
                                                stop=(c == tiles - 1 and a is at_lo))
                last.then_inc(product_done, 1)

            def fold(i, s, g):
                r = g % 2
                pe.wait_ge(pt_copied, step_count(i, s, g))
                if (s, g) == (LINEAR, 0):
                    pe.wait_ge(setup_done, SETUP_STEPS)
                    pe.wait_ge(eyes_done, len(EYES))
                if s == XT:
                    pe.wait_ge(part_done, part_count(i, CHEB0, g))
                    for u in range(tiles // 2):
                        last = nc.tensor.matmul(folded[g][:, 2 * u:2 * u + 2, feat:wide],
                                                pt_sb[r][:, u * P:(u + 1) * P], fold_v0[:, :],
                                                start=False, stop=False, skip_group_check=True)
                    last.then_inc(fold_done, 1)
                    return
                for t in range(tiles):
                    if s == MEAN:
                        last = nc.tensor.transpose(folded[g][:, t, :], pt_sb[r][:, t * P:(t + 1) * P],
                                                   ident[:, :])
                        continue
                    last = nc.tensor.matmul(folded[g][:, t, :], pt_sb[r][:, t * P:(t + 1) * P],
                                            fold_m[s][:, :],
                                            start=(t == 0 and s not in (CHEB1, CHEB2)),
                                            stop=(t == tiles - 1), skip_group_check=True)
                last.then_inc(fold_done, 1)

            def turn_slot(g):
                for c in range(tiles):
                    turn(0, g * tiles + c, first_banks)

            pe.wait_ge(ident_done, 1)
            pe.wait_ge(weights_loaded, 16 * 8)
            nc.tensor.transpose(pt[1][:, 0:feat], w1_rows[:, :], ident[0:feat, 0:feat]).then_inc(w1_turned, 1)
            turn_slot(0)
            turn_slot(1)
            product(0, MEAN, 0)
            fold(0, MEAN, 0)
            turn_slot(2)
            pe.wait_ge(w1_copied, 1)
            product(0, MEAN, 1)
            fold(0, MEAN, 1)
            turn_slot(3)
            product(0, MEAN, 2)
            product(0, MEAN, 3)
            fold(0, MEAN, 2)

            def group(i, last_group):
                before = (i, MEAN, SLOTS - 1)
                for step in steps_of(i, last_group):
                    product(*step)
                    job = job_at(*step[1:], last_group)
                    if job is not None:
                        turn(i + 1, job)
                    fold(*before)
                    before = step
                if last_group:
                    fold(*before)

            with pe.Fori(0, groups - 1) as i:
                group(i, False)
            group(groups - 1, True)

        @block.scalar
        def _(act):
            def turned_hi(p, job, banks=turned):
                g, c = job // tiles, job % tiles
                act.wait_ge(turned_done, job_count(p, job))
                nc.scalar.activation(at_hi[:, p % 2, g, c, :], banks[job % len(banks)][:, :],
                                     ACT.Copy).then_inc(at_hi_done, 1)

            def sum_rows(p, job):
                g, t = job // tiles, job % tiles
                if t == 0:
                    act.wait_ge(a_loaded[g], 16 * p + 16)
                if g == 0 and t == 0 and not isinstance(p, int):
                    act.wait_ge(stats_done, p * SLOTS)
                    act.wait_ge(inv_d_done, p * SLOTS)
                if not (isinstance(p, int) and p == 0 and job == 0):
                    act.wait_ge(rows_summed, job_count(p, job) - 1)
                nc.scalar.activation(summed[:, :], a_rows[g][:, t, :], ACT.Copy,
                                     accum_out=rowsum[:, job:job + 1]).then_inc(rows_summed, 1)

            def copy_pt(i, s, g):
                r = g % 2
                act.wait_ge(product_done, step_count(i, s, g))
                if not isinstance(i, int) or s != MEAN or g >= 2:
                    act.wait_ge(fold_done, step_count(i, s, g) - 2)
                n = nodes if s != XT else tiles // 2 * P
                nc.scalar.activation(pt_sb[r][:, 0:n], pt[r][:, 0:n], ACT.Copy).then_inc(pt_copied, 1)

            def square_y(i, s, g):
                act.wait_ge(y_done, norm_count(i, s, g))
                nc.scalar.activation(square[:, :, :], y[g][:, :, :], ACT.Square,
                                     scale=feat ** -0.5).then_inc(squared, 1)

            def hi_first(p, g):
                act.wait_ge(centred_done, slot_count(p, g))
                if not isinstance(p, int):
                    act.wait_ge(product_done, step_count(p - 1, CONV, g))
                nc.scalar.activation(operand[g][:, :, 0:feat], centred[g][:, :, :],
                                     ACT.Copy).then_inc(hi_done, 1)

            def hi(i, s, g):
                if s == LINEAR:
                    act.wait_ge(dx_done, slot_count(i, g))
                    src = dx[g]
                elif s in (CHEB0, CHEB1):
                    act.wait_ge(cheb_done, cheb_count(i, s, g))
                    src = xf[g]
                else:
                    act.wait_ge(norm_done, norm_count(i, s, g))
                    src = xf[g]
                act.wait_ge(product_done, step_count(i, s, g))
                nc.scalar.activation(operand[g][:, :, 0:feat], src[:, :, :], ACT.Copy).then_inc(hi_done, 1)

            def hi_slot(g):
                hi_first(0, g)
                for c in range(tiles):
                    turned_hi(0, g * tiles + c, first_banks)

            def sum_slot(g, rows=range(tiles)):
                for t in rows:
                    sum_rows(0, g * tiles + t)

            hi_slot(0)
            sum_slot(0)
            hi_slot(1)
            copy_pt(0, MEAN, 0)
            sum_slot(1)
            hi_slot(2)
            square_y(0, MEAN, 0)
            copy_pt(0, MEAN, 1)
            sum_slot(2, (0, 1))
            hi_slot(3)
            hi(0, MEAN, 0)
            sum_slot(2, (2, 3))
            copy_pt(0, MEAN, 2)
            square_y(0, MEAN, 1)
            sum_slot(3, (0, 1))
            copy_pt(0, MEAN, 3)
            hi(0, MEAN, 1)
            sum_slot(3, (2, 3))
            square_y(0, MEAN, 2)

            def group(i, last_group):
                steps_now = steps_of(i, last_group)

                def incoming(n):
                    copy_pt(*steps_now[n])
                    job = job_at(*steps_now[n][1:], last_group)
                    if job is not None:
                        turned_hi(i + 1, job)

                incoming(0)
                square_y(i, MEAN, SLOTS - 1)
                hi(i, MEAN, SLOTS - 2)
                incoming(1)
                before = (i, MEAN, SLOTS - 1)
                for n, step in enumerate(steps_now if last_group else steps_now[:-1]):
                    _, s, g = step
                    if s in NORMS:
                        square_y(*step)
                    if before[1] in FEEDS:
                        hi(*before)
                    if s == CONV and not last_group:
                        hi_first(i + 1, g)
                    job = job_at(s, g, last_group, SUM_STAGES)
                    if job is not None:
                        sum_rows(i + 1, job)
                    if n + 2 < len(steps_now):
                        incoming(n + 2)
                    before = step

            with act.Fori(0, groups - 1) as i:
                group(i, False)
            group(groups - 1, True)

        @block.vector
        def _(dve):
            count = [0]

            def setup(ins):
                count[0] += 1
                ins.then_inc(setup_done, 1)
                dve.wait_ge(setup_done, count[0])

            def sum_feat(p, g):
                dve.wait_ge(x_loaded[g], 16 * p + 16)
                nc.vector.tensor_reduce(cols_of(feat_sum, g), centred[g][:, :, :], AX.X, ALU.add)\
                    .then_inc(feat_summed, 1)

            def centre(p, g):
                dve.wait_ge(feat_summed, slot_count(p, g))
                nc.vector.scalar_tensor_tensor(centred[g][:, :, :], by_row(feat_sum, g), -1.0 / feat,
                                               centred[g][:, :, :], ALU.mult, ALU.add)\
                    .then_inc(centred_done, 1)

            def lo_first(p, g):
                dve.wait_ge(hi_done, operand_count(p, MEAN, g))
                nc.vector.tensor_tensor(operand[g][:, :, feat:wide], centred[g][:, :, :],
                                        operand[g][:, :, 0:feat].bitcast(F32), ALU.subtract)\
                    .then_inc(lo_done, 1)

            def turned_lo(p, job, banks=turned):
                g, c = job // tiles, job % tiles
                dve.wait_ge(at_hi_done, job_count(p, job))
                nc.vector.tensor_tensor(at_lo[:, p % 2, g, c, :], banks[job % len(banks)][:, :],
                                        at_hi[:, p % 2, g, c, :].bitcast(F32), ALU.subtract)\
                    .then_inc(at_lo_done, 1)

            def invert(p, g):
                dve.wait_ge(rows_summed, job_count(p, g * tiles + tiles - 1))
                nc.vector.tensor_scalar(cols_of(clipped, g), cols_of(rowsum, g), 1.0, None, ALU.max)\
                    .then_inc(clip_done, 1)
                nc.vector.reciprocal(cols_of(inv_sum, g), cols_of(rowsum, g))
                dve.wait_ge(clip_done, slot_count(p, g))
                nc.vector.reciprocal(cols_of(inv_deg, g), cols_of(clipped, g)).then_inc(stats_done, 1)

            def read_fold(i, s, g):
                own = folded[g][:, :, 0:feat]
                if (s, g) == (CHEB2, 0):
                    dve.wait_ge(cheb_done, cheb_count(i, CHEB1, SLOTS - 1))
                elif s == CHEB1 or s == CHEB0 and g > 0:
                    dve.wait_ge(cheb_done, cheb_count(i, s, g) - 1)
                elif s in (MEAN, CHEB2) and g > 0:
                    dve.wait_ge(y_done, norm_count(i, s, g) - 1)
                dve.wait_ge(fold_done, step_count(i, s, g))
                if s == MEAN:
                    nc.vector.tensor_reduce(hi_plus_lo[:, :, :],
                                            folded[g].rearrange("p t (h f) -> p t f h", h=2), AX.X,
                                            ALU.add).then_inc(halves_added, 1)
                    dve.wait_ge(halves_added, slot_count(i, g))
                    dve.wait_ge(stats_done, slot_count(i, g))
                    nc.vector.tensor_tensor(part[:, :, :], hi_plus_lo[:, :, :], by_row(inv_deg, g),
                                            ALU.mult).then_inc(part_done, 1)
                    residual = centred[g]
                elif s in (CHEB0, CHEB1):
                    factor = -1.0 if s == CHEB0 else -2.0
                    nc.vector.scalar_tensor_tensor(part[:, :, :], own, factor, by_row(inv_sum, g),
                                                   ALU.mult, ALU.mult).then_inc(part_done, 1)
                    dve.wait_ge(part_done, part_count(i, s, g))
                    if s == CHEB0:
                        dve.wait_ge(biased_done, biased_count(i, LINEAR, g))
                        dve.wait_ge(over_d_done, slot_count(i, g))
                    nc.vector.tensor_tensor(xf[g][:, :, :], part[:, :, :], dx[g][:, :, :], ALU.add)\
                        .then_inc(cheb_done, 1)
                    return
                elif s == CHEB2:
                    nc.vector.scalar_tensor_tensor(part[:, :, :], folded[g][:, :, feat:wide], -1.0,
                                                   by_row(d, g), ALU.mult, ALU.mult).then_inc(part_done, 1)
                    residual = xb[g]
                elif s == LINEAR:
                    residual = xf[g]
                else:
                    dve.wait_ge(biased_done, biased_count(i, CHEB2, g))
                    residual = xb[g]
                if s in (MEAN, CHEB2):
                    dve.wait_ge(part_done, part_count(i, s, g))
                    own = part[:, :, :]
                nc.vector.tensor_tensor(y[g][:, :, :], own, residual[:, :, :], ALU.add)\
                    .then_inc(y_done, 1)

            def sum_squares(i, s, g):
                dve.wait_ge(squared, norm_count(i, s, g))
                nc.vector.tensor_reduce(cols_of(variance, g), square[:, :, :], AX.X, ALU.add)\
                    .then_inc(variance_done, 1)

            def normalise(i, s, g):
                dve.wait_ge(rstd_done, norm_count(i, s, g))
                if s == MEAN:
                    dve.wait_ge(xf_free[g], 16 * i + 16)
                nc.vector.tensor_tensor(xf[g][:, :, :], y[g][:, :, :], by_row(rstd, g), ALU.mult)\
                    .then_inc(norm_done, 1)
                if s == LINEAR:
                    dve.wait_ge(norm_done, norm_count(i, s, g))
                    dve.wait_ge(d_done, slot_count(i, g))
                    nc.vector.tensor_tensor(dx[g][:, :, :], xf[g][:, :, :], by_row(d, g), ALU.mult)\
                        .then_inc(dx_done, 1)

            def lo(i, s, g):
                dve.wait_ge(hi_done, operand_count(i, FEEDS[s], g))
                src = dx[g] if s == LINEAR else xf[g]
                nc.vector.tensor_tensor(operand[g][:, :, feat:wide], src[:, :, :],
                                        operand[g][:, :, 0:feat].bitcast(F32), ALU.subtract)\
                    .then_inc(lo_done, 1)

            for g in range(SLOTS):
                nc.vector.memset(xf[g][:, 0, 0:1], 0.0).then_inc(xf_free[g], 16)
            setup(nc.vector.memset(minus_half[:, :], -0.5))
            setup(nc.vector.memset(eps[:, :], EPS))
            for s in (LINEAR, CONV):
                setup(nc.vector.memset(fold_m[s][:, feat:wide], 0.0))
            setup(nc.vector.memset(fold_v0[:, :], 0.0))
            dve.wait_ge(ident_done, 1)
            for s in EYES:
                nc.vector.tensor_tensor(fold_m[s][:, 0:feat], ident[:, 0:feat], ident[:, feat:wide],
                                        ALU.add).then_inc(eyes_done, 1)

            sum_feat(0, 0)
            centre(0, 0)
            dve.wait_ge(weights_loaded, 16 * 8)
            w1_t = fold_m[LINEAR][:, 0:feat]
            dve.wait_ge(w1_turned, 1)
            nc.vector.tensor_copy(w1_t, pt[1][:, 0:feat]).then_inc(w1_copied, 1)
            dve.wait_ge(w1_copied, 1)
            w3_c = fold_m[CONV][:, 0:feat]
            nc.vector.tensor_reduce(w_sum[:, 0:4], w2_sb[:, :, :], AX.X, ALU.add)
            nc.vector.tensor_reduce(w_sum[:, 4:5], w1_t, AX.X, ALU.add)
            nc.vector.tensor_reduce(w_sum[:, 5:6], w3_c, AX.X, ALU.add)
            nc.vector.tensor_reduce(w_sum[:, 6:7], b2_sb[:, 0, :], AX.X, ALU.add)
            setup(nc.vector.tensor_reduce(w_sum[:, 7:8], b3_sb[:, 0, :], AX.X, ALU.add))
            setup(nc.vector.scalar_tensor_tensor(w2_sb[:, :, :], w_sum[:, 0:4].unsqueeze(2).broadcast_to([P, 4, feat]),
                                                 -1.0 / feat, w2_sb[:, :, :], ALU.mult, ALU.add))
            for n, w in enumerate((w1_t, w3_c, b2_sb[:, 0, :], b3_sb[:, 0, :])):
                setup(nc.vector.scalar_tensor_tensor(w, w_sum[:, 4 + n:5 + n].broadcast_to([P, feat]),
                                                     -1.0 / feat, w, ALU.mult, ALU.add))
            w_k = [w2_sb[:, k, :] for k in range(4)]
            v1, v2, v3 = (fold_m[s][:, feat:wide] for s in (CHEB0, CHEB1, CHEB2))
            setup(nc.vector.tensor_scalar(v3, w_k[3], 2.0, None, ALU.mult))
            setup(nc.vector.scalar_tensor_tensor(v2, w_k[3], 2.0, w_k[2], ALU.mult, ALU.add))
            setup(nc.vector.tensor_scalar(v2, v2, 2.0, None, ALU.mult))
            setup(nc.vector.scalar_tensor_tensor(w_tmp[:, 0, :], w_k[3], 3.0, w_k[1], ALU.mult, ALU.add))
            setup(nc.vector.scalar_tensor_tensor(v1, w_k[2], 2.0, w_tmp[:, 0, :], ALU.mult, ALU.add))
            setup(nc.vector.tensor_tensor(w_tmp[:, 0, :], w_k[0], w_k[1], ALU.add))
            setup(nc.vector.tensor_tensor(w_tmp[:, 1, :], w_k[2], w_k[3], ALU.add))
            for h in range(2):
                rows = slice(h * feat, (h + 1) * feat)
                ins = nc.vector.scalar_tensor_tensor(fold_v0[rows, rows], w_tmp[rows, 0, :], -1.0,
                                                     w_tmp[rows, 1, :], ALU.mult, ALU.subtract)
            setup(ins)
            assert count[0] == SETUP_STEPS, count[0]

            def split_first(g, columns=range(tiles)):
                for c in columns:
                    turned_lo(0, g * tiles + c, first_banks)

            lo_first(0, 0)
            split_first(0)
            sum_feat(0, 1)
            centre(0, 1)
            invert(0, 0)
            lo_first(0, 1)
            split_first(1)
            sum_feat(0, 2)
            centre(0, 2)
            read_fold(0, MEAN, 0)
            lo_first(0, 2)
            split_first(2)
            sum_feat(0, 3)
            centre(0, 3)
            sum_squares(0, MEAN, 0)
            invert(0, 1)
            lo_first(0, 3)
            split_first(3, (0, 1))
            normalise(0, MEAN, 0)
            split_first(3, (2, 3))
            lo(0, MEAN, 0)
            read_fold(0, MEAN, 1)
            invert(0, 2)
            sum_squares(0, MEAN, 1)
            read_fold(0, MEAN, 2)
            normalise(0, MEAN, 1)
            lo(0, MEAN, 1)
            sum_squares(0, MEAN, 2)
            invert(0, 3)
            read_fold(0, MEAN, 3)
            normalise(0, MEAN, 2)
            sum_squares(0, MEAN, 3)
            lo(0, MEAN, 2)

            def group(i, last_group):
                steps_now = steps_of(i, last_group)

                def split_job(n):
                    if n < len(steps_now):
                        job = job_at(*steps_now[n][1:], last_group)
                        if job is not None:
                            turned_lo(i + 1, job)

                split_job(0)
                before = (i, MEAN, SLOTS - 1)
                for n, step in enumerate(steps_now):
                    _, s, g = step
                    if s != XT:
                        read_fold(*step)
                    if before[1] in NORMS:
                        normalise(*before)
                    if s in NORMS:
                        sum_squares(*step)
                    if before[1] in FEEDS:
                        lo(*before)
                    if before[1] == CONV and not last_group:
                        lo_first(i + 1, before[2])
                    split_job(n + 1)
                    if s == CHEB2 and not last_group:
                        sum_feat(i + 1, g)
                        centre(i + 1, g)
                    if s == CONV and not last_group:
                        invert(i + 1, g)
                    before = step
                if last_group:
                    normalise(*before)

            with dve.Fori(0, groups - 1) as i:
                group(i, False)
            group(groups - 1, True)

        @block.gpsimd
        def _(pool):
            nc.gpsimd.memset(ident[:, :], 0.0).then_inc(ident_started, 1)
            pool.wait_ge(ident_started, 1)
            nc.gpsimd.affine_select(out=ident[:, :], in_=ident[:, :], compare_op=ALU.not_equal, fill=1.0,
                                    base=0, pattern=[[-1, P]], channel_multiplier=1).then_inc(ident_done, 1)

            def root(p, g):
                pool.wait_ge(rows_summed, job_count(p, g * tiles + tiles - 1))
                if not isinstance(p, int):
                    pool.wait_ge(part_done, part_count(p - 1, CHEB2, g))
                nc.gpsimd.tensor_tensor(cols_of(d, g), cols_of(rowsum, g), cols_of(minus_half, g),
                                        ALU.pow).then_inc(d_done, 1)
                pool.wait_ge(d_done, slot_count(p, g))
                nc.gpsimd.tensor_tensor(cols_of(inv_d, g), cols_of(rowsum, g), cols_of(d, g),
                                        ALU.mult).then_inc(inv_d_done, 1)

            def root_var(i, s, g):
                pool.wait_ge(variance_done, norm_count(i, s, g))
                nc.gpsimd.tensor_tensor(cols_of(var_eps, g), cols_of(variance, g), cols_of(eps, g),
                                        ALU.add).then_inc(var_done, 1)
                pool.wait_ge(var_done, norm_count(i, s, g))
                nc.gpsimd.tensor_tensor(cols_of(rstd, g), cols_of(var_eps, g), cols_of(minus_half, g),
                                        ALU.pow).then_inc(rstd_done, 1)

            def add_bias(i, s, g):
                bias = b2_sb if s == LINEAR else b3_sb
                if (s, g) == (LINEAR, 0):
                    pool.wait_ge(setup_done, SETUP_STEPS)
                pool.wait_ge(norm_done, norm_count(i, s, g))
                nc.gpsimd.tensor_tensor(xb[g][:, :, :], xf[g][:, :, :], bias[:, :, :].broadcast_to([P, tiles, feat]),
                                        ALU.add).then_inc(biased_done, 1)

            def over_d(i, g):
                pool.wait_ge(norm_done, norm_count(i, LINEAR, g))
                pool.wait_ge(inv_d_done, slot_count(i, g))
                nc.gpsimd.tensor_tensor(x_over_d[g][:, :, :], xf[g][:, :, :], by_row(inv_d, g), ALU.mult)\
                    .then_inc(over_d_done, 1)

            pool.wait_ge(setup_done, 2)
            root(0, 0)
            root(0, 1)
            root_var(0, MEAN, 0)
            root(0, 2)
            root_var(0, MEAN, 1)
            root_var(0, MEAN, 2)
            root_var(0, MEAN, 3)
            root(0, 3)

            def group(i, last_group):
                before = (i, MEAN, SLOTS - 1)
                for step in steps_of(i, last_group):
                    _, s, g = step
                    if before[1] == LINEAR:
                        over_d(i, before[2])
                    if before[1] in (LINEAR, CHEB2):
                        add_bias(*before)
                    if s in NORMS:
                        root_var(*step)
                    if s == CONV and not last_group:
                        root(i + 1, g)
                    before = step

            with pool.Fori(0, groups - 1) as i:
                group(i, False)
            group(groups - 1, True)


_INS = ['x', 'adj', 'L1_gnn_W', 'L2_gnn_weight', 'L2_gnn_bias', 'L3_gnn_weight', 'L3_gnn_bias']
_OUTS = [((16, 512, 64), 'float32')]


def kernel(**inputs):
    import numpy as _np
    import concourse.bacc as _bacc
    from concourse import mybir as _mybir
    from concourse.bass_utils import run_bass_kernel_spmd as _run

    nc = _bacc.Bacc("TRN2", target_bir_lowering=False, num_devices=1)
    arrays, args = {}, []
    for name in _INS:
        a = _np.ascontiguousarray(inputs[name])
        arrays[f"in_{name}_dram"] = a
        args.append(nc.dram_tensor(f"in_{name}_dram", a.shape, _mybir.dt.from_np(a.dtype), kind="ExternalInput").ap())
    for i, (shape, dtype) in enumerate(_OUTS):
        dt = _mybir.dt.from_np(_np.dtype(dtype))
        args.append(nc.dram_tensor(f"out_{i}_dram", shape, dt, kind="ExternalOutput").ap())
    resnorm_kernel(nc, *args)
    r = _run(nc, [arrays], core_ids=[0])
    got = tuple(r.results[0][f"out_{i}_dram"] for i in range(len(_OUTS)))
    return got[0]
```

```python
import concourse.bass as bass
from concourse import mybir
from contextlib import ExitStack

F32 = mybir.dt.float32
F32R = mybir.dt.float32r
BF16 = mybir.dt.bfloat16
ALU = mybir.AluOpType
ACT = mybir.ActivationFunctionType
AX = mybir.AxisListType

SLOTS = 4
EPS = 1e-5
MEAN, LINEAR, CHEB0, XT, CHEB1, CHEB2, CONV = range(7)
STAGES = (MEAN, LINEAR, CHEB0, XT, CHEB1, CHEB2, CONV)
NORMS = (MEAN, LINEAR, CHEB2, CONV)
PARTS = (MEAN, CHEB0, CHEB1, CHEB2)
FEEDS = {MEAN: LINEAR, LINEAR: CHEB0, CHEB0: CHEB1, CHEB1: CHEB2, CHEB2: CONV}

PASS = [(LINEAR, 0), (LINEAR, 1), (LINEAR, 2), (LINEAR, 3),
        (CHEB0, 0), (CHEB0, 1), (XT, 0), (CHEB0, 2), (XT, 1), (CHEB0, 3),
        (CHEB1, 0), (XT, 2), (CHEB1, 1), (XT, 3), (CHEB1, 2), (CHEB1, 3),
        (CHEB2, 0), (CHEB2, 1), (CHEB2, 2), (CHEB2, 3),
        (CONV, 0), (CONV, 1), (MEAN, 0), (CONV, 2), (MEAN, 1), (CONV, 3), (MEAN, 2), (MEAN, 3)]
LAST_PASS = [step for step in PASS if step[0] != MEAN]
JOB_STEPS = [step for step in PASS if step[0] in (LINEAR, CHEB0, CHEB1)] \
    + [(CONV, 0), (CONV, 1), (MEAN, 0), (CONV, 2)]
FIRST_STEPS = [(CHEB2, 3), (CONV, 0), (MEAN, 0), (CONV, 2)]
FIRST = 7
HANDED = []
for before, step in zip(PASS[-1:] + PASS[:-1], PASS):
    HANDED += [before] if before[0] in FEEDS else []
    HANDED += [(FIRST, FIRST_STEPS.index(step))] if step in FIRST_STEPS else []
HANDED = HANDED[1:] + HANDED[:1]
SUM_STEPS = [step for step in PASS if step[0] in (LINEAR, CHEB0, CHEB1, CHEB2)]


def resnorm_kernel(nc, x, adj, w1, w2, b2, w3, b3, out):
    graphs, nodes, feat = x.shape
    P = 128
    tiles = nodes // P
    jobs = SLOTS * tiles
    groups = graphs // SLOTS
    wide = 2 * feat
    assert wide == P and graphs % SLOTS == 0

    a_view = adj.rearrange("b (t p) m -> b p t m", p=P)
    x_view = x.rearrange("b (t p) f -> b p t f", p=P)
    out_view = out.rearrange("b (t p) f -> b p t f", p=P)

    ctx = ExitStack()
    with ctx:
        def sb(name, shape, dt=F32):
            return ctx.enter_context(nc.sbuf_tensor(name, shape, dt))

        def sem(name):
            return ctx.enter_context(nc.semaphore(name))

        a_rows = [sb(f"a_rows{g}", [P, tiles, nodes]) for g in range(SLOTS)]
        at_hi = sb("at_hi", [P, 2, SLOTS, tiles, nodes], F32R)
        at_lo = sb("at_lo", [P, 2, SLOTS, tiles, nodes], F32R)
        centred = [sb(f"centred{g}", [P, tiles, feat]) for g in range(SLOTS)]
        xf = [sb(f"xf{g}", [P, tiles, feat]) for g in range(SLOTS)]
        xb = [sb(f"xb{g}", [P, tiles, feat]) for g in range(SLOTS)]
        x_over_d = [sb(f"x_over_d{g}", [P, tiles, feat]) for g in range(SLOTS)]
        dx = [sb(f"dx{g}", [P, tiles, feat]) for g in range(SLOTS)]
        operand = [sb(f"operand{g}", [P, tiles, wide], F32R) for g in range(SLOTS)]
        y = [sb(f"y{g}", [P, tiles, feat]) for g in range(SLOTS)]
        part = sb("part", [P, tiles, feat])
        hi_plus_lo = sb("hi_plus_lo", [P, tiles, feat])
        square = sb("square", [P, tiles, feat + 1])
        pt_sb = [sb(f"pt_sb{r}", [P, nodes]) for r in range(2)]
        summed = sb("summed", [P, nodes], BF16)
        cols = SLOTS * tiles
        rowsum = sb("rowsum", [P, cols])
        clipped = sb("clipped", [P, cols])
        inv_deg = sb("inv_deg", [P, cols])
        inv_sum = sb("inv_sum", [P, cols])
        d = sb("d", [P, cols])
        inv_d = sb("inv_d", [P, cols])
        feat_sum = sb("feat_sum", [P, cols])
        var_eps = sb("var_eps", [P, cols])
        rstd = sb("rstd", [P, cols])
        minus_half = sb("minus_half", [P, cols])
        ident = sb("ident", [P, P])
        fold_m = {s: sb(f"fold_m{s}", [P, wide]) for s in FEEDS.values()}
        fold_v0 = sb("fold_v0", [P, wide])
        w1_rows = sb("w1_rows", [feat, wide])
        w2_sb = sb("w2_sb", [P, 4, feat])
        b2_sb = sb("b2_sb", [P, 1, feat])
        b3_sb = sb("b3_sb", [P, 1, feat])
        w_sum = sb("w_sum", [P, 8])
        w_tmp = sb("w_tmp", [P, 4, feat])

        pt = [ctx.enter_context(nc.psum_tensor(f"pt{r}", [P, nodes], F32)) for r in range(2)]
        turned = [ctx.enter_context(nc.psum_tensor(f"turned{r}", [P, nodes], F32)) for r in range(2)]
        folded_banks = [ctx.enter_context(nc.psum_tensor(f"folded{g}", [P, nodes], F32))
                        for g in range(SLOTS)]
        folded = [bank[:, :].rearrange("p (t c) -> p t c", c=wide) for bank in folded_banks]

        first_banks = (turned[0], turned[1], folded_banks[2], folded_banks[3])

        a_loaded = [sem(f"a_loaded{g}") for g in range(SLOTS)]
        x_loaded = [sem(f"x_loaded{g}") for g in range(SLOTS)]
        xf_free = [sem(f"xf_free{g}") for g in range(SLOTS)]
        a_first_half = sem("a_first_half")
        weights_loaded = sem("weights_loaded")
        turned_done = sem("turned_done")
        product_done = sem("product_done")
        fold_done = sem("fold_done")
        w1_turned = sem("w1_turned")
        at_hi_done = sem("at_hi_done")
        rows_summed = sem("rows_summed")
        pt_copied = sem("pt_copied")
        squared = sem("squared")
        hi_done = sem("hi_done")
        at_lo_done = sem("at_lo_done")
        feat_summed = sem("feat_summed")
        centred_done = sem("centred_done")
        halves_added = sem("halves_added")
        part_done = sem("part_done")
        y_done = sem("y_done")
        cheb_done = sem("cheb_done")
        variance_done = sem("variance_done")
        norm_done = sem("norm_done")
        dx_done = sem("dx_done")
        lo_done = sem("lo_done")
        clip_done = sem("clip_done")
        stats_done = sem("stats_done")
        w1_copied = sem("w1_copied")
        eyes_done = sem("eyes_done")
        constants_set = sem("constants_set")
        sums_done = sem("sums_done")
        weights_centred = sem("weights_centred")
        terms_done = sem("terms_done")
        folds_set = sem("folds_set")
        ident_started = sem("ident_started")
        ident_done = sem("ident_done")
        rstd_done = sem("rstd_done")
        biased_done = sem("biased_done")
        over_d_done = sem("over_d_done")
        d_done = sem("d_done")
        inv_d_done = sem("inv_d_done")

        def is_first_mean(i, s):
            return s == MEAN and isinstance(i, int) and i == 0

        def pass_of(i, s):
            at = i - 1 if s == MEAN else i
            return at, LAST_PASS if isinstance(at, int) and at == groups - 1 else PASS

        def count_in_order(i, s, g, stages):
            if is_first_mean(i, s):
                return g + 1
            at, order = pass_of(i, s)
            index = [step for step in order if step[0] in stages].index((s, g))
            return at * sum(step[0] in stages for step in PASS) + SLOTS + index + 1

        def step_count(i, s, g):
            return count_in_order(i, s, g, STAGES)

        def bank_of(i, s, g):
            return g % 2 if is_first_mean(i, s) else pass_of(i, s)[1].index((s, g)) % 2

        def norm_count(i, s, g):
            return count_in_order(i, s, g, NORMS)

        def part_count(i, s, g):
            return count_in_order(i, s, g, PARTS)

        before_stage = {LINEAR: MEAN, CHEB0: LINEAR, CHEB1: CHEB0, CHEB2: CHEB1, CONV: CHEB2}

        def handed_count(i, s, g):
            if is_first_mean(i, s):
                return SLOTS + g + 1
            at, order = pass_of(i, s)
            handed = HANDED if order is PASS else [source for source in HANDED if source in LAST_PASS]
            return at * len(HANDED) + 2 * SLOTS + handed.index((s, g)) + 1

        def operand_count(i, s, g):
            if s == MEAN:
                return g + 1 if is_first_mean(i, s) else handed_count(i - 1, FIRST, g)
            source = before_stage[s]
            if s == LINEAR and HANDED.index((MEAN, g)) < HANDED.index((FIRST, SLOTS - 1)):
                return handed_count(i, MEAN, g) + (HANDED.index((FIRST, SLOTS - 1)) - HANDED.index((MEAN, g)))
            return handed_count(i, source, g)

        def cheb_count(i, s, g):
            return i * (2 * SLOTS) + (s == CHEB1) * SLOTS + g + 1

        def biased_count(i, s, g):
            return i * (2 * SLOTS) + (s == CHEB2) * SLOTS + g + 1

        def slot_count(i, g):
            return i * SLOTS + g + 1

        def job_count(i, job):
            return i * jobs + job + 1

        def cols_of(t, g):
            return t[:, g * tiles:(g + 1) * tiles]

        def by_row(t, g):
            return cols_of(t, g).unsqueeze(2).broadcast_to([P, tiles, feat])

        def steps_of(i, last_group):
            return [(i + 1 if s == MEAN else i, s, g) for s, g in (LAST_PASS if last_group else PASS)]

        def job_at(s, g, last_group, carriers=JOB_STEPS):
            if last_group or (s, g) not in carriers:
                return None
            return carriers.index((s, g))

        EYES = (CHEB0, CHEB1, CHEB2)

        block = ctx.enter_context(nc.Block())

        @block.sync
        def _(sp):
            def load_a(p, g):
                sp.dma_start(a_rows[g][:, :, :], a_view[p * SLOTS + g]).then_inc(a_loaded[g], 16)

            def load_x(p, g):
                sp.dma_start(centred[g][:, :, :], x_view[p * SLOTS + g]).then_inc(x_loaded[g], 16)

            def reload_a(p, slots=range(SLOTS)):
                for g in slots:
                    sp.wait_ge(turned_done, job_count(p - 1, g * tiles + tiles - 1))
                    sp.wait_ge(rows_summed, job_count(p - 1, g * tiles + tiles - 1))
                    load_a(p, g)

            def reload_x(p):
                sp.wait_ge(y_done, norm_count(p - 1, MEAN, SLOTS - 1))
                for g in range(SLOTS):
                    load_x(p, g)

            def store(i, slots=range(SLOTS)):
                for g in slots:
                    sp.wait_ge(norm_done, norm_count(i, CONV, g))
                    sp.dma_start(out_view[i * SLOTS + g], xf[g][:, :, :]).then_inc(xf_free[g], 16)

            def load_weights():
                sp.dma_start(w1_rows[:, 0:feat], w1).then_inc(weights_loaded, 16)
                sp.dma_start(w1_rows[:, feat:wide], w1).then_inc(weights_loaded, 16)
                for half in (0, feat):
                    sp.dma_start(w2_sb[half:half + feat, :, :],
                                  w2.rearrange("k o c d -> c (k o) d")).then_inc(weights_loaded, 16)
                    sp.dma_start(fold_m[CONV][half:half + feat, 0:feat], w3).then_inc(weights_loaded, 16)
                sp.dma_start(b2_sb[:, 0, :], b2[0, 0, :].partition_broadcast(P)).then_inc(weights_loaded, 16)
                sp.dma_start(b3_sb[:, 0, :], b3.partition_broadcast(P)).then_inc(weights_loaded, 16)

            half = nodes // 2
            sp.dma_start(a_rows[0][:, :, 0:half], a_view[0, :, :, 0:half]).then_inc(a_first_half, 16)
            load_x(0, 0)
            sp.dma_start(a_rows[0][:, :, half:nodes], a_view[0, :, :, half:nodes]).then_inc(a_loaded[0], 16)
            load_weights()
            for g in range(1, SLOTS):
                load_x(0, g)
                load_a(0, g)
            reload_a(1)
            with sp.Fori(0, groups - 2) as i:
                reload_x(i + 1)
                reload_a(i + 2, range(SLOTS - 1))
                store(i, range(SLOTS - 1))
                reload_a(i + 2, (SLOTS - 1,))
                store(i, (SLOTS - 1,))
            reload_x(groups - 1)
            store(groups - 2)
            store(groups - 1)
            for g in range(SLOTS):
                sp.wait_ge(xf_free[g], 16 * groups + 16)

        @block.tensor
        def _(pe):
            def turn(p, job, banks=turned):
                g, c = job // tiles, job % tiles
                bank = banks[job % len(banks)]
                if isinstance(p, int) and g == 0:
                    pe.wait_ge(a_first_half if c < tiles // 2 else a_loaded[0], 16)
                elif c == 0:
                    pe.wait_ge(a_loaded[g], 16 * p + 16)
                if not isinstance(p, int) or job >= len(banks):
                    pe.wait_ge(at_lo_done, job_count(p, job) - len(banks))
                for t in range(tiles):
                    last = nc.tensor.transpose(bank[:, t * P:(t + 1) * P],
                                               a_rows[g][:, t, c * P:(c + 1) * P], ident[:, :])
                last.then_inc(turned_done, 1)

            def product(i, s, g):
                r = bank_of(i, s, g)
                if not isinstance(i, int) or s != MEAN or g >= 2:
                    pe.wait_ge(pt_copied, step_count(i, s, g) - 2)
                if s == XT:
                    pe.wait_ge(over_d_done, slot_count(i, g))
                    for u in range(tiles // 2):
                        last = nc.tensor.transpose(pt[r][:, u * P:(u + 1) * P],
                                                   x_over_d[g][:, 2 * u:2 * u + 2, :], ident[:, :])
                    last.then_inc(product_done, 1)
                    return
                if s == MEAN:
                    pe.wait_ge(at_lo_done, job_count(i, g * tiles + tiles - 1))
                pe.wait_ge(lo_done, operand_count(i, s, g))
                for c in range(tiles):
                    for a in (at_hi, at_lo):
                        last = nc.tensor.matmul(pt[r][:, :], operand[g][:, c, :], a[:, i % 2, g, c, :],
                                                start=(c == 0 and a is at_hi),
                                                stop=(c == tiles - 1 and a is at_lo))
                last.then_inc(product_done, 1)

            def fold(i, s, g):
                r = bank_of(i, s, g)
                pe.wait_ge(pt_copied, step_count(i, s, g))
                if (s, g) == (LINEAR, 0):
                    pe.wait_ge(weights_centred, 5)
                    pe.wait_ge(terms_done, 5)
                    pe.wait_ge(folds_set, 4)
                    pe.wait_ge(eyes_done, len(EYES))
                if s == XT:
                    pe.wait_ge(part_done, part_count(i, CHEB0, g))
                    for u in range(tiles // 2):
                        last = nc.tensor.matmul(folded[g][:, 2 * u:2 * u + 2, feat:wide],
                                                pt_sb[r][:, u * P:(u + 1) * P], fold_v0[:, :],
                                                start=False, stop=False, skip_group_check=True)
                    last.then_inc(fold_done, 1)
                    return
                if s == MEAN and not is_first_mean(i, s):
                    pe.wait_ge(y_done, norm_count(i - 1, CONV, g))
                for t in range(tiles):
                    if s == MEAN:
                        last = nc.tensor.transpose(folded[g][:, t, :], pt_sb[r][:, t * P:(t + 1) * P],
                                                   ident[:, :])
                        continue
                    last = nc.tensor.matmul(folded[g][:, t, :], pt_sb[r][:, t * P:(t + 1) * P],
                                            fold_m[s][:, :],
                                            start=(t == 0 and s not in (CHEB1, CHEB2)),
                                            stop=(t == tiles - 1), skip_group_check=True)
                last.then_inc(fold_done, 1)

            def keep_busy(bank, products):
                for _ in range(products):
                    nc.tensor.transpose(bank[:, 0:P], ident[:, :], ident[:, :])

            def turn_slot(g):
                for c in range(tiles):
                    turn(0, g * tiles + c, first_banks)

            pe.wait_ge(ident_done, 1)
            keep_busy(pt[0], 14)
            turn_slot(0)
            pe.wait_ge(weights_loaded, 16 * 8)
            nc.tensor.transpose(pt[1][:, 0:feat], w1_rows[:, :], ident[0:feat, 0:feat]).then_inc(w1_turned, 1)
            keep_busy(pt[0], 30)
            turn_slot(1)
            product(0, MEAN, 0)
            fold(0, MEAN, 0)
            turn_slot(2)
            pe.wait_ge(w1_copied, 1)
            product(0, MEAN, 1)
            fold(0, MEAN, 1)
            turn_slot(3)
            product(0, MEAN, 2)
            product(0, MEAN, 3)
            fold(0, MEAN, 2)

            def group(i, last_group):
                before = (i, MEAN, SLOTS - 1)
                for step in steps_of(i, last_group):
                    product(*step)
                    job = job_at(*step[1:], last_group)
                    if job is not None:
                        turn(i + 1, job)
                    fold(*before)
                    before = step
                if last_group:
                    fold(*before)

            with pe.Fori(0, groups - 1) as i:
                group(i, False)
            group(groups - 1, True)

        @block.scalar
        def _(act):
            def turned_hi(p, job, banks=turned):
                g, c = job // tiles, job % tiles
                act.wait_ge(turned_done, job_count(p, job))
                nc.scalar.activation(at_hi[:, p % 2, g, c, :], banks[job % len(banks)][:, :],
                                     ACT.Copy).then_inc(at_hi_done, 1)

            def sum_rows(p, job):
                g, t = job // tiles, job % tiles
                if isinstance(p, int) and job == 0:
                    act.wait_ge(a_first_half, 16)
                if t == 0:
                    act.wait_ge(a_loaded[g], 16 * p + 16)
                if g == 0 and t == 0 and not isinstance(p, int):
                    act.wait_ge(stats_done, p * SLOTS)
                    act.wait_ge(inv_d_done, p * SLOTS)
                if not (isinstance(p, int) and p == 0 and job == 0):
                    act.wait_ge(rows_summed, job_count(p, job) - 1)
                nc.scalar.activation(summed[:, :], a_rows[g][:, t, :], ACT.Copy,
                                     accum_out=rowsum[:, job:job + 1]).then_inc(rows_summed, 1)

            def copy_pt(i, s, g):
                r = bank_of(i, s, g)
                act.wait_ge(product_done, step_count(i, s, g))
                if not isinstance(i, int) or s != MEAN or g >= 2:
                    act.wait_ge(fold_done, step_count(i, s, g) - 2)
                n = nodes if s != XT else tiles // 2 * P
                nc.scalar.activation(pt_sb[r][:, 0:n], pt[r][:, 0:n], ACT.Copy).then_inc(pt_copied, 1)

            def square_y(i, s, g):
                act.wait_ge(y_done, norm_count(i, s, g))
                nc.scalar.activation(square[:, :, 0:feat], y[g][:, :, :], ACT.Square,
                                     scale=feat ** -0.5).then_inc(squared, 1)

            def hi_first(p, g):
                act.wait_ge(centred_done, slot_count(p, g))
                if not isinstance(p, int):
                    act.wait_ge(product_done, step_count(p - 1, CONV, g))
                nc.scalar.activation(operand[g][:, :, 0:feat], centred[g][:, :, :],
                                     ACT.Copy).then_inc(hi_done, 1)

            def hi(i, s, g):
                if s == LINEAR:
                    act.wait_ge(dx_done, slot_count(i, g))
                    src = dx[g]
                elif s in (CHEB0, CHEB1):
                    act.wait_ge(cheb_done, cheb_count(i, s, g))
                    src = xf[g]
                else:
                    act.wait_ge(norm_done, norm_count(i, s, g))
                    src = xf[g]
                act.wait_ge(product_done, step_count(i, s, g))
                nc.scalar.activation(operand[g][:, :, 0:feat], src[:, :, :], ACT.Copy).then_inc(hi_done, 1)

            def hi_slot(g):
                hi_first(0, g)
                for c in range(tiles):
                    turned_hi(0, g * tiles + c, first_banks)

            def sum_slot(g, rows=range(tiles)):
                for t in rows:
                    sum_rows(0, g * tiles + t)

            hi_slot(0)
            sum_slot(0)
            hi_slot(1)
            copy_pt(0, MEAN, 0)
            sum_slot(1)
            hi_slot(2)
            square_y(0, MEAN, 0)
            copy_pt(0, MEAN, 1)
            sum_slot(2, (0,))
            hi_slot(3)
            sum_slot(2, (1,))
            hi(0, MEAN, 0)
            sum_slot(2, (2, 3))
            copy_pt(0, MEAN, 2)
            square_y(0, MEAN, 1)
            sum_slot(3, (0, 1))
            copy_pt(0, MEAN, 3)
            square_y(0, MEAN, 2)
            hi(0, MEAN, 1)
            sum_slot(3, (2, 3))

            def group(i, last_group):
                steps_now = steps_of(i, last_group)

                def incoming(n):
                    copy_pt(*steps_now[n])
                    job = job_at(*steps_now[n][1:], last_group)
                    if job is not None:
                        turned_hi(i + 1, job)

                incoming(0)
                hi(i, MEAN, SLOTS - 2)
                square_y(i, MEAN, SLOTS - 1)
                incoming(1)
                before = (i, MEAN, SLOTS - 1)
                for n, step in enumerate(steps_now if last_group else steps_now[:-1]):
                    _, s, g = step
                    if s in NORMS and s not in PARTS:
                        square_y(*step)
                    if before[1] in FEEDS:
                        hi(*before)
                    slot = job_at(s, g, last_group, FIRST_STEPS)
                    if slot is not None:
                        hi_first(i + 1, slot)
                    if s in NORMS and s in PARTS:
                        square_y(*step)
                    if n + 2 < len(steps_now):
                        incoming(n + 2)
                    job = job_at(s, g, last_group, SUM_STEPS)
                    if job is not None:
                        sum_rows(i + 1, job)
                    before = step

            with act.Fori(0, groups - 1) as i:
                group(i, False)
            group(groups - 1, True)

        @block.vector
        def _(dve):
            def sum_feat(p, g):
                dve.wait_ge(x_loaded[g], 16 * p + 16)
                nc.vector.tensor_reduce(cols_of(feat_sum, g), centred[g][:, :, :], AX.X, ALU.add)\
                    .then_inc(feat_summed, 1)

            def centre(p, g):
                dve.wait_ge(feat_summed, slot_count(p, g))
                nc.vector.scalar_tensor_tensor(centred[g][:, :, :], by_row(feat_sum, g), -1.0 / feat,
                                               centred[g][:, :, :], ALU.mult, ALU.add)\
                    .then_inc(centred_done, 1)

            def lo_first(p, g):
                dve.wait_ge(hi_done, operand_count(p, MEAN, g))
                nc.vector.tensor_tensor(operand[g][:, :, feat:wide], centred[g][:, :, :],
                                        operand[g][:, :, 0:feat].bitcast(F32), ALU.subtract)\
                    .then_inc(lo_done, 1)

            def turned_lo(p, job, banks=turned):
                g, c = job // tiles, job % tiles
                dve.wait_ge(at_hi_done, job_count(p, job))
                nc.vector.tensor_tensor(at_lo[:, p % 2, g, c, :], banks[job % len(banks)][:, :],
                                        at_hi[:, p % 2, g, c, :].bitcast(F32), ALU.subtract)\
                    .then_inc(at_lo_done, 1)

            def invert(p, slots):
                first, last = slots[0], slots[-1]
                own = slice(first * tiles, (last + 1) * tiles)
                dve.wait_ge(rows_summed, job_count(p, last * tiles + tiles - 1))
                nc.vector.tensor_scalar(clipped[:, own], rowsum[:, own], 1.0, None, ALU.max)\
                    .then_inc(clip_done, len(slots))
                nc.vector.reciprocal(inv_sum[:, own], rowsum[:, own])
                dve.wait_ge(clip_done, slot_count(p, last))
                nc.vector.reciprocal(inv_deg[:, own], clipped[:, own]).then_inc(stats_done, len(slots))

            def add_halves(i, g):
                if g > 0:
                    dve.wait_ge(y_done, norm_count(i, MEAN, g - 1))
                dve.wait_ge(fold_done, step_count(i, MEAN, g))
                nc.vector.tensor_reduce(hi_plus_lo[:, :, :], folded[g].rearrange("p t (h f) -> p t f h", h=2),
                                        AX.X, ALU.add).then_inc(halves_added, 1)

            def scale(i, s, g):
                if s == MEAN:
                    dve.wait_ge(halves_added, slot_count(i, g))
                    dve.wait_ge(stats_done, slot_count(i, g))
                    nc.vector.tensor_tensor(part[:, :, :], hi_plus_lo[:, :, :], by_row(inv_deg, g),
                                            ALU.mult).then_inc(part_done, 1)
                    return
                if s == CHEB2 and g > 0:
                    dve.wait_ge(y_done, norm_count(i, CHEB2, g - 1))
                elif (s, g) != (CHEB0, 0):
                    last = (s, g - 1) if g > 0 else (before_stage[s], SLOTS - 1)
                    dve.wait_ge(cheb_done, cheb_count(i, *last))
                dve.wait_ge(fold_done, step_count(i, s, g))
                if s == CHEB2:
                    nc.vector.scalar_tensor_tensor(part[:, :, :], folded[g][:, :, feat:wide], -1.0,
                                                   by_row(d, g), ALU.mult, ALU.mult).then_inc(part_done, 1)
                else:
                    nc.vector.scalar_tensor_tensor(part[:, :, :], folded[g][:, :, 0:feat],
                                                   -1.0 if s == CHEB0 else -2.0,
                                                   by_row(inv_sum, g), ALU.mult, ALU.mult)\
                        .then_inc(part_done, 1)

            def add_residual(i, s, g):
                if s in PARTS:
                    dve.wait_ge(part_done, part_count(i, s, g))
                    own = part[:, :, :]
                else:
                    dve.wait_ge(fold_done, step_count(i, s, g))
                    own = folded[g][:, :, 0:feat]
                if s in (CHEB0, CHEB1):
                    if s == CHEB0:
                        dve.wait_ge(biased_done, biased_count(i, LINEAR, g))
                        dve.wait_ge(over_d_done, slot_count(i, g))
                    nc.vector.tensor_tensor(xf[g][:, :, :], own, dx[g][:, :, :], ALU.add)\
                        .then_inc(cheb_done, 1)
                    return
                if s == CONV:
                    dve.wait_ge(biased_done, biased_count(i, CHEB2, g))
                residual = {MEAN: centred, LINEAR: xf, CHEB2: xb, CONV: xb}[s][g]
                nc.vector.tensor_tensor(y[g][:, :, :], own, residual[:, :, :], ALU.add)\
                    .then_inc(y_done, 1)

            def sum_squares(i, s, g):
                dve.wait_ge(squared, norm_count(i, s, g))
                nc.vector.tensor_reduce(cols_of(var_eps, g), square[:, :, :], AX.X, ALU.add)\
                    .then_inc(variance_done, 1)

            def normalise(i, s, g):
                dve.wait_ge(rstd_done, norm_count(i, s, g))
                if s == MEAN:
                    dve.wait_ge(xf_free[g], 16 * i + 16)
                nc.vector.tensor_tensor(xf[g][:, :, :], y[g][:, :, :], by_row(rstd, g), ALU.mult)\
                    .then_inc(norm_done, 1)
                if s == LINEAR:
                    dve.wait_ge(norm_done, norm_count(i, s, g))
                    dve.wait_ge(d_done, slot_count(i, g))
                    nc.vector.tensor_tensor(dx[g][:, :, :], xf[g][:, :, :], by_row(d, g), ALU.mult)\
                        .then_inc(dx_done, 1)

            def lo(i, s, g):
                dve.wait_ge(hi_done, handed_count(i, s, g))
                src = dx[g] if s == LINEAR else xf[g]
                nc.vector.tensor_tensor(operand[g][:, :, feat:wide], src[:, :, :],
                                        operand[g][:, :, 0:feat].bitcast(F32), ALU.subtract)\
                    .then_inc(lo_done, 1)

            def set_up_constants():
                for g in range(SLOTS):
                    nc.vector.memset(xf[g][:, 0, 0:1], 0.0).then_inc(xf_free[g], 16)
                nc.vector.memset(minus_half[:, :], -0.5).then_inc(constants_set, 1)
                nc.vector.memset(square[:, :, feat:feat + 1], EPS).then_inc(constants_set, 1)
                for s in (LINEAR, CONV):
                    nc.vector.memset(fold_m[s][:, feat:wide], 0.0).then_inc(constants_set, 1)
                nc.vector.memset(fold_v0[:, :], 0.0).then_inc(constants_set, 1)
                dve.wait_ge(ident_done, 1)
                for s in EYES:
                    nc.vector.tensor_tensor(fold_m[s][:, 0:feat], ident[:, 0:feat], ident[:, feat:wide],
                                            ALU.add).then_inc(eyes_done, 1)

            def set_up_weights():
                dve.wait_ge(weights_loaded, 16 * 8)
                dve.wait_ge(w1_turned, 1)
                w1_t = fold_m[LINEAR][:, 0:feat]
                nc.vector.tensor_copy(w1_t, pt[1][:, 0:feat]).then_inc(w1_copied, 1)
                w3_c = fold_m[CONV][:, 0:feat]
                nc.vector.tensor_reduce(w_sum[:, 0:4], w2_sb[:, :, :], AX.X, ALU.add).then_inc(sums_done, 1)
                singles = (w3_c, b2_sb[:, 0, :], b3_sb[:, 0, :], w1_t)
                for n, w in enumerate(singles):
                    if w is w1_t:
                        dve.wait_ge(w1_copied, 1)
                    nc.vector.tensor_reduce(w_sum[:, 4 + n:5 + n], w, AX.X, ALU.add).then_inc(sums_done, 1)
                dve.wait_ge(sums_done, 5)
                nc.vector.scalar_tensor_tensor(w2_sb[:, :, :], w_sum[:, 0:4].unsqueeze(2).broadcast_to([P, 4, feat]),
                                               -1.0 / feat, w2_sb[:, :, :], ALU.mult, ALU.add)\
                    .then_inc(weights_centred, 1)
                for n, w in enumerate(singles):
                    nc.vector.scalar_tensor_tensor(w, w_sum[:, 4 + n:5 + n].broadcast_to([P, feat]),
                                                   -1.0 / feat, w, ALU.mult, ALU.add).then_inc(weights_centred, 1)
                w_k = [w2_sb[:, k, :] for k in range(4)]
                v1, v2, v3 = (fold_m[s][:, feat:wide] for s in (CHEB0, CHEB1, CHEB2))
                dve.wait_ge(weights_centred, 1)
                nc.vector.tensor_scalar(v3, w_k[3], 2.0, None, ALU.mult).then_inc(terms_done, 1)
                nc.vector.tensor_scalar(w_tmp[:, 0, :], w_k[2], 2.0, None, ALU.mult).then_inc(terms_done, 1)
                nc.vector.scalar_tensor_tensor(w_tmp[:, 1, :], w_k[3], 3.0, w_k[1], ALU.mult, ALU.add)\
                    .then_inc(terms_done, 1)
                nc.vector.tensor_tensor(w_tmp[:, 2, :], w_k[0], w_k[1], ALU.add).then_inc(terms_done, 1)
                nc.vector.tensor_tensor(w_tmp[:, 3, :], w_k[2], w_k[3], ALU.add).then_inc(terms_done, 1)
                dve.wait_ge(terms_done, 5)
                dve.wait_ge(constants_set, 5)
                nc.vector.scalar_tensor_tensor(v2, w_k[3], 4.0, w_tmp[:, 0, :], ALU.mult, ALU.add)\
                    .then_inc(folds_set, 1)
                nc.vector.tensor_tensor(v1, w_tmp[:, 0, :], w_tmp[:, 1, :], ALU.add).then_inc(folds_set, 1)
                for h in range(2):
                    rows = slice(h * feat, (h + 1) * feat)
                    nc.vector.scalar_tensor_tensor(fold_v0[rows, rows], w_tmp[rows, 2, :], -1.0,
                                                   w_tmp[rows, 3, :], ALU.mult, ALU.subtract)\
                        .then_inc(folds_set, 1)

            set_up_constants()
            sum_feat(0, 0)
            centre(0, 0)

            def split_first(g, columns=range(tiles)):
                for c in columns:
                    turned_lo(0, g * tiles + c, first_banks)

            lo_first(0, 0)
            split_first(0)
            set_up_weights()
            sum_feat(0, 1)
            centre(0, 1)
            invert(0, (0,))
            lo_first(0, 1)
            split_first(1)
            sum_feat(0, 2)
            centre(0, 2)
            add_halves(0, 0)
            scale(0, MEAN, 0)
            add_residual(0, MEAN, 0)
            sum_feat(0, 3)
            centre(0, 3)
            lo_first(0, 2)
            split_first(2)
            sum_squares(0, MEAN, 0)
            invert(0, (1,))
            lo_first(0, 3)
            split_first(3, (0, 1))
            normalise(0, MEAN, 0)
            split_first(3, (2, 3))
            lo(0, MEAN, 0)
            add_halves(0, 1)
            scale(0, MEAN, 1)
            add_residual(0, MEAN, 1)
            sum_squares(0, MEAN, 1)
            invert(0, (2,))
            add_halves(0, 2)
            scale(0, MEAN, 2)
            add_residual(0, MEAN, 2)
            normalise(0, MEAN, 1)
            sum_squares(0, MEAN, 2)
            lo(0, MEAN, 1)
            add_halves(0, 3)
            invert(0, (3,))
            normalise(0, MEAN, 2)
            scale(0, MEAN, 3)
            add_residual(0, MEAN, 3)
            lo(0, MEAN, 2)
            sum_squares(0, MEAN, 3)

            def group(i, last_group):
                steps_now = steps_of(i, last_group)

                def split_job(n):
                    if n < len(steps_now):
                        job = job_at(*steps_now[n][1:], last_group)
                        if job is not None:
                            turned_lo(i + 1, job)

                split_job(0)
                before = (i, MEAN, SLOTS - 1)
                for n, step in enumerate(steps_now):
                    _, s, g = step
                    next_mean = n + 1 < len(steps_now) and steps_now[n + 1][1] == MEAN
                    if s in PARTS:
                        scale(*step)
                    residual_first = s not in (CHEB0, CHEB1, CHEB2) and not s == before[1] == MEAN
                    if residual_first and s != XT:
                        add_residual(*step)
                    closing = last_group and (s, g) == (CONV, SLOTS - 1)
                    if closing:
                        sum_squares(*step)
                    if before[1] in NORMS:
                        normalise(*before)
                    if not residual_first:
                        add_residual(*step)
                    if s in (LINEAR, CONV) and not closing:
                        sum_squares(*step)
                    if next_mean and before[1] == MEAN:
                        add_halves(i + 1, steps_now[n + 1][2])
                    if before[1] in FEEDS:
                        lo(*before)
                    slot = job_at(s, g, last_group, FIRST_STEPS)
                    if slot is not None:
                        lo_first(i + 1, slot)
                    if s in (CHEB2, MEAN):
                        sum_squares(*step)
                    split_job(n + 1)
                    if next_mean and before[1] != MEAN:
                        add_halves(i + 1, steps_now[n + 1][2])
                    if s == XT and not last_group:
                        sum_feat(i + 1, g)
                        centre(i + 1, g)
                    if (s, g) == (CONV, 1) and not last_group:
                        invert(i + 1, range(SLOTS))
                    before = step
                if last_group:
                    normalise(*before)

            with dve.Fori(0, groups - 1) as i:
                group(i, False)
            group(groups - 1, True)

        @block.gpsimd
        def _(pool):
            nc.gpsimd.memset(ident[:, :], 0.0).then_inc(ident_started, 1)
            pool.wait_ge(ident_started, 1)
            nc.gpsimd.affine_select(out=ident[:, :], in_=ident[:, :], compare_op=ALU.not_equal, fill=1.0,
                                    base=0, pattern=[[-1, P]], channel_multiplier=1).then_inc(ident_done, 1)

            def root(p, g):
                pool.wait_ge(rows_summed, job_count(p, g * tiles + tiles - 1))
                if not isinstance(p, int):
                    pool.wait_ge(part_done, part_count(p - 1, CHEB2, g))
                nc.gpsimd.tensor_tensor(cols_of(d, g), cols_of(rowsum, g), cols_of(minus_half, g),
                                        ALU.pow).then_inc(d_done, 1)
                pool.wait_ge(d_done, slot_count(p, g))
                nc.gpsimd.tensor_tensor(cols_of(inv_d, g), cols_of(rowsum, g), cols_of(d, g),
                                        ALU.mult).then_inc(inv_d_done, 1)

            def root_var(i, s, g):
                pool.wait_ge(variance_done, norm_count(i, s, g))
                nc.gpsimd.tensor_tensor(cols_of(rstd, g), cols_of(var_eps, g), cols_of(minus_half, g),
                                        ALU.pow).then_inc(rstd_done, 1)

            def add_bias(i, s, g):
                bias = b2_sb if s == LINEAR else b3_sb
                if (s, g) == (LINEAR, 0):
                    pool.wait_ge(weights_centred, 5)
                pool.wait_ge(norm_done, norm_count(i, s, g))
                nc.gpsimd.tensor_tensor(xb[g][:, :, :], xf[g][:, :, :], bias[:, :, :].broadcast_to([P, tiles, feat]),
                                        ALU.add).then_inc(biased_done, 1)

            def over_d(i, g):
                pool.wait_ge(norm_done, norm_count(i, LINEAR, g))
                pool.wait_ge(inv_d_done, slot_count(i, g))
                nc.gpsimd.tensor_tensor(x_over_d[g][:, :, :], xf[g][:, :, :], by_row(inv_d, g), ALU.mult)\
                    .then_inc(over_d_done, 1)

            pool.wait_ge(constants_set, 1)
            root(0, 0)
            root(0, 1)
            root_var(0, MEAN, 0)
            root(0, 2)
            root_var(0, MEAN, 1)
            root_var(0, MEAN, 2)
            root_var(0, MEAN, 3)
            root(0, 3)

            def group(i, last_group):
                before = (i, MEAN, SLOTS - 1)
                for step in steps_of(i, last_group):
                    _, s, g = step
                    if before[1] == LINEAR:
                        over_d(i, before[2])
                    if before[1] in (LINEAR, CHEB2):
                        add_bias(*before)
                    if s in NORMS:
                        root_var(*step)
                    if s == CONV and not last_group:
                        root(i + 1, g)
                    before = step

            with pool.Fori(0, groups - 1) as i:
                group(i, False)
            group(groups - 1, True)


_INS = ['x', 'adj', 'L1_gnn_W', 'L2_gnn_weight', 'L2_gnn_bias', 'L3_gnn_weight', 'L3_gnn_bias']
_OUTS = [((16, 512, 64), 'float32')]


def kernel(**inputs):
    import numpy as _np
    import concourse.bacc as _bacc
    from concourse import mybir as _mybir
    from concourse.bass_utils import run_bass_kernel_spmd as _run

    nc = _bacc.Bacc("TRN2", target_bir_lowering=False, num_devices=1)
    arrays, args = {}, []
    for name in _INS:
        a = _np.ascontiguousarray(inputs[name])
        arrays[f"in_{name}_dram"] = a
        args.append(nc.dram_tensor(f"in_{name}_dram", a.shape, _mybir.dt.from_np(a.dtype), kind="ExternalInput").ap())
    for i, (shape, dtype) in enumerate(_OUTS):
        dt = _mybir.dt.from_np(_np.dtype(dtype))
        args.append(nc.dram_tensor(f"out_{i}_dram", shape, dt, kind="ExternalOutput").ap())
    resnorm_kernel(nc, *args)
    r = _run(nc, [arrays], core_ids=[0])
    got = tuple(r.results[0][f"out_{i}_dram"] for i in range(len(_OUTS)))
    return got[0]
```
